# Optimizing a Trainium2 kernel written in Bass

```python
import numpy as np
import jax
import jax.numpy as jnp

def _softmax(x, axis=-1):
    return jax.nn.softmax(x, axis=axis)

def _gelu(x):
    return jax.nn.gelu(x, approximate=True)

def _silu(x):
    return jax.nn.silu(x)

def _sigmoid(x):
    return jax.nn.sigmoid(x)

def _layernorm(x, axis=-1, eps=1e-05):
    m = jnp.mean(x, axis=axis, keepdims=True)
    v = jnp.var(x, axis=axis, keepdims=True)
    return (x - m) / jnp.sqrt(v + eps)

def _scatter_add(tgt, idx, src, axis=0):
    return tgt.at[idx].add(src)

def _segment_sum(src, seg, n):
    return jax.ops.segment_sum(src, seg, n)
kernel_name = 'mk_hybrid_d1_jaxref_r8_787530'

def setup_inputs(seed: int=0):
    np.random.seed(seed)
    _w = jnp.asarray

    def _L0_attn_a_setup():
        import jax, jax.numpy as jnp
        import numpy as np
        HEADS = 16
        DIM_HEAD = 64
        key = jax.random.key(seed)
        k1, k2, k3, k4 = jax.random.split(key, 4)
        B, T, D = (4, 128, 128)
        x = jax.random.normal(k1, (B, T, D), dtype=jnp.float32)
        w_qkv = jax.random.normal(k2, (3 * HEADS * DIM_HEAD, D), dtype=jnp.float32) * (1.0 / np.sqrt(D))
        w_out = jax.random.normal(k3, (D, HEADS * DIM_HEAD), dtype=jnp.float32) * (1.0 / np.sqrt(HEADS * DIM_HEAD))
        rel_bias = jax.random.normal(k4, (2 * 128 - 1, HEADS), dtype=jnp.float32) * 0.02
        return {'x': x, 'w_qkv': w_qkv, 'w_out': w_out, 'rel_bias': rel_bias}
    _L0_attn_a_in = _L0_attn_a_setup()

    def _L0_attn_b_setup():
        import jax, jax.numpy as jnp
        import numpy as np
        B, T, C = (64, 32, 128)
        N_HEAD, HEAD_SIZE, KV_RANK = (16, 64, 128)
        BLOCK_SIZE = 32
        key = jax.random.key(seed)
        ks = jax.random.split(key, 5)
        HD = N_HEAD * HEAD_SIZE

        def init(k, shape):
            fan_in = shape[0]
            bound = 1.0 / np.sqrt(fan_in)
            return jax.random.uniform(k, shape, jnp.float32, -bound, bound)
        return {'x': jax.random.normal(ks[0], (B, T, C), jnp.float32), 'w_kv_down': init(ks[1], (C, KV_RANK)), 'w_kv_up': init(ks[2], (KV_RANK, 2 * HD)), 'w_q': init(ks[3], (C, HD)), 'w_out': init(ks[4], (HD, C))}
    _L0_attn_b_in = _L0_attn_b_setup()

    def _L0_ffn_setup():
        import jax, jax.numpy as jnp
        import numpy as np
        B, S, D, F, E = (4, 256, 128, 512, 8)
        LN_EPS = 1e-05
        key = jax.random.key(seed)
        ks = jax.random.split(key, 6)
        sc = 0.02
        return {'x': jax.random.normal(ks[0], (B, S, D), dtype=jnp.float32), 'Wr': jax.random.normal(ks[1], (D, E), dtype=jnp.float32) * sc, 'br': jnp.zeros((E,), jnp.float32), 'ln_g': jnp.ones((D,), jnp.float32), 'ln_b': jnp.zeros((D,), jnp.float32), 'W1': jax.random.normal(ks[2], (E, D, F), dtype=jnp.float32) * sc, 'b1': jnp.zeros((E, F), jnp.float32), 'W2': jax.random.normal(ks[3], (E, F, D), dtype=jnp.float32) * sc, 'b2': jnp.zeros((E, D), jnp.float32)}
    _L0_ffn_in = _L0_ffn_setup()
    _d = {'L0_attn_a_x': _L0_attn_a_in['x'], 'L0_attn_a_w_qkv': _L0_attn_a_in['w_qkv'], 'L0_attn_a_w_out': _L0_attn_a_in['w_out'], 'L0_attn_a_rel_bias': _L0_attn_a_in['rel_bias'], 'L0_attn_b_w_kv_down': _L0_attn_b_in['w_kv_down'], 'L0_attn_b_w_kv_up': _L0_attn_b_in['w_kv_up'], 'L0_attn_b_w_q': _L0_attn_b_in['w_q'], 'L0_attn_b_w_out': _L0_attn_b_in['w_out'], 'L0_ffn_Wr': _L0_ffn_in['Wr'], 'L0_ffn_br': _L0_ffn_in['br'], 'L0_ffn_ln_g': _L0_ffn_in['ln_g'], 'L0_ffn_ln_b': _L0_ffn_in['ln_b'], 'L0_ffn_W1': _L0_ffn_in['W1'], 'L0_ffn_b1': _L0_ffn_in['b1'], 'L0_ffn_W2': _L0_ffn_in['W2'], 'L0_ffn_b2': _L0_ffn_in['b2']}
    _x0 = _d['L0_attn_a_x']
    _d['L0_attn_a_x'] = jax.random.normal(jax.random.fold_in(jax.random.key(seed), 1), (8, 256, 128), dtype=_x0.dtype)
    del _x0
    return _d

def reference(L0_attn_a_x, L0_attn_a_w_qkv, L0_attn_a_w_out, L0_attn_a_rel_bias, L0_attn_b_w_kv_down, L0_attn_b_w_kv_up, L0_attn_b_w_q, L0_attn_b_w_out, L0_ffn_Wr, L0_ffn_br, L0_ffn_ln_g, L0_ffn_ln_b, L0_ffn_W1, L0_ffn_b1, L0_ffn_W2, L0_ffn_b2):

    def _L0_attn_a_ref(x, w_qkv, w_out, rel_bias):
        import jax, jax.numpy as jnp
        import numpy as np
        HEADS = 16
        DIM_HEAD = 64
        b, t, _ = x.shape
        h, dh = (HEADS, DIM_HEAD)
        scale = dh ** (-0.5)
        qkv = x @ w_qkv.T
        qkv = qkv.reshape(b, t, dh, 3, h).transpose(3, 0, 4, 1, 2)
        q, k, v = (qkv[0], qkv[1], qkv[2])
        scores = jnp.einsum('bhid,bhjd->bhij', q, k) * scale
        rel = jnp.arange(t)[None, :] - jnp.arange(t)[:, None] + (t - 1)
        bias = rel_bias[rel]
        scores = scores + bias.transpose(2, 0, 1)[None]
        attn = jax.nn.softmax(scores, axis=-1)
        out = jnp.einsum('bhij,bhjd->bhid', attn, v)
        out = out.transpose(0, 2, 1, 3).reshape(b, t, h * dh)
        return out @ w_out.T

    def _L0_attn_b_ref(x, w_kv_down, w_kv_up, w_q, w_out):
        import jax, jax.numpy as jnp
        import numpy as np
        B, T, C = (64, 32, 128)
        N_HEAD, HEAD_SIZE, KV_RANK = (16, 64, 128)
        BLOCK_SIZE = 32
        Bx, Tx, Cx = x.shape
        HD = N_HEAD * HEAD_SIZE
        latent_kv = x @ w_kv_down
        kv = latent_kv @ w_kv_up
        k, v = (kv[..., :HD], kv[..., HD:])
        k = k.reshape(Bx, Tx, N_HEAD, HEAD_SIZE)
        v = v.reshape(Bx, Tx, N_HEAD, HEAD_SIZE)
        q = (x @ w_q).reshape(Bx, Tx, N_HEAD, HEAD_SIZE)
        scale = HEAD_SIZE ** (-0.5)
        att = jnp.einsum('bqhd,bkhd->bhqk', q, k) * scale
        causal = jnp.tril(jnp.ones((Tx, Tx), dtype=bool))
        att = jnp.where(causal, att, -jnp.inf)
        att = jax.nn.softmax(att, axis=-1)
        y = jnp.einsum('bhqk,bkhd->bqhd', att, v)
        y = y.reshape(Bx, Tx, HD)
        return y @ w_out

    def _L0_ffn_ref(x, Wr, br, ln_g, ln_b, W1, b1, W2, b2):
        import jax, jax.numpy as jnp
        import numpy as np
        B, S, D, F, E = (4, 256, 128, 512, 8)
        LN_EPS = 1e-05
        tokens_shape = x.shape[:-1]
        xt = x.reshape(-1, x.shape[-1])
        router_logits = xt @ Wr + br
        router_probs = jax.nn.softmax(router_logits, axis=-1)
        gates = jnp.max(router_probs, axis=-1, keepdims=True)
        idx = jnp.argmax(router_probs, axis=-1)
        onehot = jax.nn.one_hot(idx, E, dtype=xt.dtype)
        mu = jnp.mean(xt, axis=-1, keepdims=True)
        var = jnp.mean(jnp.square(xt - mu), axis=-1, keepdims=True)
        xn = (xt - mu) * jax.lax.rsqrt(var + LN_EPS) * ln_g + ln_b
        h = jnp.einsum('te,td,edf->tf', onehot, xn, W1) + b1[idx]
        h = jax.nn.relu(h)
        y = jnp.einsum('te,tf,efd->td', onehot, h, W2) + b2[idx]
        y = y * gates
        return y.reshape(tokens_shape + (y.shape[-1],))
    x = L0_attn_a_x
    x = x + _L0_attn_a_ref(_layernorm(x, axis=-1), L0_attn_a_w_qkv, L0_attn_a_w_out, L0_attn_a_rel_bias)
    x = x + _L0_ffn_ref(_layernorm(x, axis=-1), L0_ffn_Wr, L0_ffn_br, L0_ffn_ln_g, L0_ffn_ln_b, L0_ffn_W1, L0_ffn_b1, L0_ffn_W2, L0_ffn_b2)
    x = x + _L0_attn_b_ref(_layernorm(x, axis=-1), L0_attn_b_w_kv_down, L0_attn_b_w_kv_up, L0_attn_b_w_q, L0_attn_b_w_out)
    x = x + _L0_ffn_ref(_layernorm(x, axis=-1), L0_ffn_Wr, L0_ffn_br, L0_ffn_ln_g, L0_ffn_ln_b, L0_ffn_W1, L0_ffn_b1, L0_ffn_W2, L0_ffn_b2)
    return x

_drawn_inputs = setup_inputs


def setup_inputs(seed=0):
    import zlib

    import numpy as np

    out = dict(_drawn_inputs(seed))
    spreads = {'L0_ffn_br': (0.0, 0.1),
     'L0_ffn_ln_g': (1.0, 0.6),
     'L0_ffn_ln_b': (0.0, 2.0),
     'L0_ffn_b1': (0.0, 0.725),
     'L0_ffn_b2': (0.0, 0.1)}
    factors = {'L0_attn_a_rel_bias': 29.236, 'L0_attn_b_w_q': 8.0}
    for name, (base, spread) in spreads.items():
        noise = np.random.default_rng([zlib.crc32(name.encode()), seed]).standard_normal(out[name].shape)
        drawn = base * np.exp(spread * noise) if base else spread * noise
        out[name] = jnp.asarray(drawn.astype(out[name].dtype))
    for name, factor in factors.items():
        out[name] = (out[name] * factor).astype(out[name].dtype)
    return out
```

```python
from contextlib import ExitStack

import numpy as np

import concourse.bass as bass
from concourse import mybir

F32 = mybir.dt.float32
F32R = mybir.dt.float32r
I32 = mybir.dt.int32
ALU = mybir.AluOpType
ACT = mybir.ActivationFunctionType
AX = mybir.AxisListType.X

NT = 16
NB = 8
NC = 8
NE = 8
NS = 23
EPS = 1e-5
BIG = 3.0e38
MASKED = 1.0e30


class Counter:

    def __init__(self, handle, step=1):
        self.handle, self.step, self.n = handle, step, 0

    def up(self, ins):
        ins.then_inc(self.handle, self.step)
        self.n += self.step
        return self, self.n


class Waits:

    def __init__(self):
        self.seen = {}

    def __call__(self, eng, *marks):
        for m in marks:
            if m is None:
                continue
            c, v = m
            key = (eng.engine, c)
            if self.seen.get(key, 0) < v:
                eng.wait_ge(c.handle, v)
                self.seen[key] = v


def build(nc, t):
    pe, dve, act, pool, sp = nc.tensor, nc.vector, nc.scalar, nc.gpsimd, nc.sync
    ctx = ExitStack()
    names = [0]

    def sem(name, step=1):
        return Counter(ctx.enter_context(nc.semaphore(name)), step)

    wait = Waits()
    c_pe, c_dve, c_act, c_pool = sem("c_pe"), sem("c_dve"), sem("c_act"), sem("c_pool")

    def sb(name, shape, dt=F32, scope=None):
        return (scope or ctx).enter_context(nc.sbuf_tensor(name, shape, dt))

    def dma_sem():
        names[0] += 1
        return sem(f"d{names[0]}", 16)

    def load(dst, src, eng=None, after=(), c=None):
        eng = eng or sp
        wait(eng, *after)
        c = c or dma_sem()
        return c.up(eng.dma_start(dst, src))

    ps = [ctx.enter_context(nc.psum_tensor(f"ps{i}", [128, 512], F32)) for i in range(8)]
    PT_, PX = ps[0], ps[7]
    PS = ps[1:4]
    PP = ps[4:6]
    PO = ps[6]

    xs_dram = nc.dram_tensor("xs_scratch", (NS * 128, 128), F32).ap()
    ys_dram = nc.dram_tensor("ys_scratch", (NS * 128, 128), F32).ap()

    x = sb("x", [128, NT, 128])
    w1h, w1l = sb("w1h", [128, NE * 512], F32R), sb("w1l", [128, NE * 512], F32R)
    w2h, w2l = sb("w2h", [128, NE * 512], F32R), sb("w2l", [128, NE * 512], F32R)
    b1s = sb("b1s", [128, 512], F32R)
    b2s = sb("b2s", [128, 128], F32R)
    pid = sb("pid", [128, 1])
    pidi = sb("pidi", [128, 1], I32)
    xn = sb("xn", [128, NT, 128])
    mh, ml = sb("mh", [128, 16 * 128], F32R), sb("ml", [128, 16 * 128], F32R)
    wvh, wvl = sb("wvh", [128, 1024], F32R), sb("wvl", [128, 1024], F32R)
    wo = sb("wo", [128, 8, 128])
    ident = sb("ident", [128, 128])
    tri = sb("tri", [128, 128])
    ones = sb("ones", [128, 128])
    lng, lnb = sb("lng", [128, 128]), sb("lnb", [128, 128])
    brb = sb("brb", [128, NE])
    wr = sb("wr", [128, NE])
    zero = sb("zero", [128, 128])
    half = sb("half", [128, 16])
    stats = sb("stats", [128, 2, 6])
    mv = sb("mv", [128, 2, 2])
    rstd = sb("rstd", [128, 2])
    kdh, kdl = sb("kdh", [128, 128], F32R), sb("kdl", [128, 128], F32R)
    lg = sb("lg", [128, NT, NE])

    iota_e = sb("iota_e", [128, NE])
    iota_k = sb("iota_k", [128, 16])
    iota_s = sb("iota_s", [128, NS])
    cT = sb("cT", [128, 16])

    base = ExitStack()
    a_ring = [sb(f"ring{i}", [128, 2, 2, 256], scope=base) for i in range(3)]
    a_pt = [sb(f"pt{i}", [128, 2, 512], scope=base) for i in range(2)]
    a_th = [sb(f"th{i}", [128, 512], F32R, scope=base) for i in range(2)]
    a_tl = [sb(f"tl{i}", [128, 512], F32R, scope=base) for i in range(2)]
    a_v = [sb(f"v{i}", [128, 2, 1024], scope=base) for i in range(2)]
    a_ot = sb("ot", [128, 8, 256], scope=base)
    a_xh = sb("xh", [128, 2, 128], scope=base)
    a_ph = sb("ph", [128, 2, 128], scope=base)
    a_pT = sb("pT", [128, 256], scope=base)
    a_xth = [sb(f"xth{i}", [128, 256], F32R, scope=base) for i in range(2)]
    a_xtl = [sb(f"xtl{i}", [128, 256], F32R, scope=base) for i in range(2)]
    a_lth = [sb(f"lth{i}", [128, 256], F32R, scope=base) for i in range(2)]
    a_ltl = [sb(f"ltl{i}", [128, 256], F32R, scope=base) for i in range(2)]
    a_mn = [sb(f"mn{i}", [128, 4], scope=base) for i in range(3)]
    a_sm = [sb(f"sm{i}", [128, 4], scope=base) for i in range(3)]
    a_rs = [sb(f"rs{i}", [128, 4], scope=base) for i in range(3)]
    s2 = sb("s2", [128, 2, 6], scope=base)
    m2 = sb("m2", [128, 2, 2], scope=base)
    r2 = sb("r2", [128, 2], scope=base)
    a_T = sb("T", [128, 17, 256], scope=base)
    stage = [sb(f"stage{i}", [128, 512], scope=base) for i in range(2)]
    top = dict(bytes=nc.sbuf_bytes_remaining)
    base.close()

    pre = ExitStack()
    wqn = sb("wqn", [128, 8, 128], scope=pre)
    wkn = sb("wkn", [128, 8, 128], scope=pre)
    wvn = sb("wvn", [128, 8, 128], scope=pre)
    won = sb("won", [128, 1024], scope=pre)
    pre.close()

    fs = ExitStack()
    f_xs = sb("f_xs", [128, NS, 128], scope=fs)
    f_ys = sb("f_ys", [128, NS, 128], scope=fs)
    f_xth = [sb(f"f_xth{i}", [128, 512], F32R, scope=fs) for i in range(2)]
    f_xtl = [sb(f"f_xtl{i}", [128, 512], F32R, scope=fs) for i in range(2)]
    f_h = [sb(f"f_h{i}", [128, 512], scope=fs) for i in range(2)]
    f_hth = [sb(f"f_hth{i}", [128, 512], F32R, scope=fs) for i in range(2)]
    f_htl = [sb(f"f_htl{i}", [128, 512], F32R, scope=fs) for i in range(2)]
    f_oh = [sb(f"f_oh{i}", [128, NT, NE], scope=fs) for i in range(8)]
    f_s = [sb(f"f_s{i}", [128, NT], scope=fs) for i in range(6)]
    f_e = [sb(f"f_e{i}", [128, NE], scope=fs) for i in range(6)]
    f_g = sb("f_g", [128, NS, NE], scope=fs)
    f_k16 = sb("f_k16", [128, NE, 16], scope=fs)
    f_i = sb("f_i", [128, NT], I32, scope=fs)
    f_ei = sb("f_ei", [128, NS], I32, scope=fs)
    f_ef = sb("f_ef", [128, NS], scope=fs)
    f_sel = sb("f_sel", [128, NS], F32R, scope=fs)
    bq = sb("bq", [128, 1024], scope=fs)
    bu = sb("bu", [128, 2048], scope=fs)
    bqT = sb("bqT", [128, 8, 128], scope=fs)
    bkT = sb("bkT", [128, 8, 128], scope=fs)
    bkd = sb("bkd", [128, 128], scope=fs)
    fs.close()


    xv = t["x"].rearrange("b (s p) d -> p (b s) d", p=128)
    ov = t["out"].rearrange("b (s p) d -> p (b s) d", p=128)
    d_x = load(x[:, :, :], xv)
    wq3 = t["w_qkv"].rearrange("(d c h) x -> c d h x", c=3, h=16)
    c_w = dma_sem()
    for j, w in enumerate((wqn, wkn, wvn)):
        for hh in range(2):
            d_w = load(w[64 * hh:64 * hh + 64, :, :], wq3[j, :, hh::2, :], c=c_w, eng=act if hh else sp)
    d_won = load(won[:, :], t["w_out_a"])
    d_T = load(a_T[:, 0:16, :], t["bias"], eng=act)
    d_wr = load(wr[:, :], t["Wr"])
    c_b = dma_sem()
    load(lng[:, :], t["ln_g"].rearrange("(a d) -> a d", a=1).broadcast_to((128, 128)), c=c_b)
    load(lnb[:, :], t["ln_b"].rearrange("(a d) -> a d", a=1).broadcast_to((128, 128)), c=c_b)
    d_b = load(brb[:, :], t["br"].rearrange("(a d) -> a d", a=1).broadcast_to((128, NE)), c=c_b)

    def setup(ins):
        k = c_pool.up(ins)
        wait(pool, k)
        return k

    k_z = setup(pool.memset(zero[:, :], 0.0))
    setup(pool.memset(ident[:, :], 0.0))
    k_id = setup(pool.affine_select(out=ident[:, :], in_=ident[:, :], compare_op=ALU.not_equal, fill=1.0,
                                    base=0, pattern=[[-1, 128]], channel_multiplier=1))
    k_h = setup(pool.memset(half[:, :], -0.5))
    setup(pool.memset(ones[:, :], 1.0))
    k_tri = setup(pool.affine_select(out=tri[:, :], in_=ones[:, :], compare_op=ALU.is_gt, fill=0.0,
                                     base=0, pattern=[[1, 128]], channel_multiplier=-1))
    k_T0 = setup(pool.memset(a_T[:, 16, :], 0.0))
    setup(pool.memset(b1s[:, :].bitcast(F32), 0.0))
    k_b0 = setup(pool.memset(b2s[:, :].bitcast(F32), 0.0))
    setup(pool.memset(pid[:, :], -1.0))
    for row in (0, 32):
        setup(pool.iota(pidi[row:row + NE, :], pattern=[[0, 1]], base=0, channel_multiplier=1))
        k_pid = setup(pool.tensor_copy(pid[row:row + NE, :], pidi[row:row + NE, :]))
    for e in range(NE):
        setup(pool.memset(iota_e[:, e:e + 1], float(NE - e)))
    for e in range(16):
        setup(pool.memset(iota_k[:, e:e + 1], float(128 * e)))
    for e in range(NS):
        k_iota = setup(pool.memset(iota_s[:, e:e + 1], float(e)))
    c_z = dma_sem()
    wait(act, k_z)
    for s in range(NS):
        d_zero = c_z.up(act.dma_start(xs_dram[128 * s:128 * s + 128, :], zero[:, :]))

    def split(high, low, src, after, scale=None, he=act, le=dve):
        wait(he, *after)
        cnt = {id(act): c_act, id(dve): c_dve, id(pool): c_pool}
        if he is act:
            i = act.activation(high, src, ACT.Copy, scale=1.0 if scale is None else scale)
        else:
            i = he.tensor_copy(high, src)
        a = cnt[id(he)].up(i)
        wait(le, a, *after)
        if scale is None:
            i = le.tensor_tensor(low, src, high.bitcast(F32), ALU.subtract)
        else:
            i = le.scalar_tensor_tensor(low, src, scale, high.bitcast(F32), ALU.mult, ALU.subtract)
        return a, cnt[id(le)].up(i)

    def three(out, ah, al, bh, bl, first=True, last=True):
        pe.matmul(out, ah, bh, start=first, stop=False)
        pe.matmul(out, al, bh, start=False, stop=False)
        return pe.matmul(out, ah, bl, start=False, stop=last)

    def tr(out, src):
        return pe.transpose(out, src, ident[:, :])

    def products(q, k, banks):
        marks = []
        for g in range(2):
            for hh in range(2):
                bank = banks[2 * g + hh]
                rows = slice(64 * hh, 64 * hh + 64)
                for j in range(4):
                    i = pe.matmul(bank[:, 128 * j:128 * j + 128], q[rows, 4 * g + j, :], k[rows, 4 * g + j, :],
                                  start=True, stop=True)
                m = c_pe.up(i)
                v = [w[:, :].rearrange("p (c h n) -> p h c n", h=2, n=128)[:, hh, 4 * g:4 * g + 4, :] for w in (mh, ml)]
                marks += split(*v, bank[:, :].rearrange("p (c n) -> p c n", c=4), [m], scale=-0.125)
        return marks

    free = [None] * 8
    wait(pe, d_w, k_id)
    k_m = []
    k_m += products(wqn, wkn, ps[0:4])
    for g in range(2):
        bank = ps[4 + g]
        for j in range(4):
            i = tr(bank[:, 128 * j:128 * j + 128], wvn[:, 4 * g + j, :])
        k = c_pe.up(i)
        r = slice(512 * g, 512 * g + 512)
        k_m += split(wvh[:, r], wvl[:, r], bank[:, :], [k])
    wait(pe, d_won)
    for g in range(2):
        bank = ps[6 + g]
        for j in range(4):
            i = tr(bank[:, 128 * j:128 * j + 128], won[:, 512 * g + 128 * j:512 * g + 128 * j + 128])
        k = c_pe.up(i)
        wait(act, k)
        k_m.append(c_act.up(act.copy(wo[:, 4 * g:4 * g + 4, :], bank[:, :].rearrange("p (a b) -> p a b", a=4))))
    k_wa = [c_pe, c_pe.n]
    wait(pool, d_T, k_T0)
    tc = a_T[:, 0:16, 255:256]
    wait(dve, d_T)
    k = c_dve.up(dve.tensor_copy(cT[:, :], tc.rearrange("p a b -> p (a b)")))
    wait(dve, k)
    k_T = c_dve.up(dve.tensor_tensor(a_T[:, 0:16, :], cT[:, :].rearrange("p (a b) -> p a b", b=1).broadcast_to((128, 16, 256)),
                                     a_T[:, 0:16, :], ALU.subtract))
    k_weights = k_m + [k_T, k_T0]

    stage_free = [None, None]
    chunks = []
    for e in range(NE):
        chunks.append((w1h, w1l, e, t["W1"][e]))
        chunks.append((w2h, w2l, e, t["W2"][e].rearrange("(c p) d -> p c d", p=128)))
    c_st = [dma_sem(), dma_sem()]
    k_ff = [None]

    def stage_chunk(n):
        if n >= len(chunks):
            return
        h, l, e, src = chunks[n]
        s = stage[n % 2]
        dst = s[:, :] if len(src.shape) == 2 else s[:, :].rearrange("p (c d) -> p c d", c=4)
        d = load(dst, src, after=[stage_free[n % 2]], c=c_st[n % 2])
        r = slice(512 * e, 512 * e + 512)
        _, stage_free[n % 2] = split(h[:, r], l[:, r], s[:, :], [d], he=pool, le=pool)
        k_ff[0] = stage_free[n % 2]

    def stage_bias(src, dst, w):
        s, c = stage[0], c_st[0]
        for row in (0, 32):
            d = load(s[row:row + NE, 0:w], src, after=[stage_free[0]], c=c)
        wait(pool, d, (c_pool, c_pool.n))
        setup(pool.tensor_copy(dst[0:NE, :], s[0:NE, 0:w]))
        setup(pool.tensor_copy(dst[32:32 + NE, :], s[32:32 + NE, 0:w]))
        stage_free[0] = setup(pool.tensor_tensor(dst[32:32 + NE, :], s[32:32 + NE, 0:w],
                                                     dst[32:32 + NE, :].bitcast(F32), ALU.subtract))
        k_ff[0] = stage_free[0]

    def norm(src, dst, st, m, r, after, gain=False):
        wait(dve, *after)
        for j in range(2):
            k = c_dve.up(dve.bn_stats(st[:, j, :], src[:, j, :]))
        wait(dve, k)
        for j in range(2):
            k = c_dve.up(dve.bn_aggr(m[:, j, :], st[:, j, :]))
        wait(dve, k)
        k = c_dve.up(dve.tensor_scalar(r[:, :], m[:, :, 1], EPS, None, ALU.add))
        wait(pool, k, k_h)
        k = c_pool.up(pool.tensor_tensor(r[:, :], r[:, :], half[:, 0:2], ALU.pow))
        wait(dve, k)
        for j in range(2):
            k = c_dve.up(dve.tensor_scalar(dst[:, j, :], src[:, j, :], m[:, j, 0:1], r[:, j:j + 1],
                                           ALU.subtract, ALU.mult))
        if not gain:
            return k
        wait(pool, k, d_b)
        bc = lambda a: a[:, :].rearrange("p (a d) -> p a d", a=1).broadcast_to((128, 2, 128))
        k = c_pool.up(pool.tensor_tensor(dst, dst, bc(lng), ALU.mult))
        wait(pool, k)
        return c_pool.up(pool.tensor_tensor(dst, dst, bc(lnb), ALU.add))

    def attention(stage_b, x_ready, w_ready, table, table_ready, extra):
        causal = stage_b
        xT, lT, V = {}, {}, {}
        k_T_, k_tH, k_tL, k_S, k_mn, k_exp, k_nrm, k_TR, k_PT, k_PV, k_O = ({} for _ in range(11))
        k_out, k_xh_free, k_psx, k_post = {}, [None], [None], {}
        k_x = {}
        last_T = {}

        def pre_a(b):
            k_x[b] = norm(x[:, 2 * b:2 * b + 2, :], a_xh[:, :, :], stats, mv, rstd,
                          [x_ready(b), k_xh_free[0]])

        def pre_b(b):
            wait(pe, k_x[b], k_psx[0], k_id)
            for j in range(2):
                i = tr(PX[:, 128 * j:128 * j + 128], a_xh[:, j, :])
            k = c_pe.up(i)
            k_xh_free[0] = k
            gone = [k_S.get(8 * (b - 2) + 7), k_V.get((b - 2, 3))] if not stage_b else [k_lat.get(b - 2), k_T_.get(8 * (b - 2) + 7)]
            xT[b] = split(a_xth[b % 2][:, :], a_xtl[b % 2][:, :], PX[:, 0:256], [k, *gone])
            k_psx[0] = xT[b][1]

        k_lat = {}
        k_V = {}

        def pre_c(b):
            wait(pe, *xT[b], k_psx[0], *w_ready)
            k = k_lat[b] = c_pe.up(three(PX[:, 0:256], kdh[:, :], kdl[:, :], a_xth[b % 2][:, :], a_xtl[b % 2][:, :]))
            lT[b] = split(a_lth[b % 2][:, :], a_ltl[b % 2][:, :], PX[:, 0:256],
                          [k, k_S.get(8 * (b - 2) + 7), k_V.get((b - 2, 3))])
            k_psx[0] = lT[b][1]

        def key(b):
            return (a_lth, a_ltl, lT) if stage_b else (a_xth, a_xtl, xT)

        def values(b, n):
            H, L, marks = key(b)
            j, half_ = n // 2, n % 2
            wait(pe, *marks[b], k_psx[0], *w_ready)
            r = slice(512 * half_, 512 * half_ + 512)
            c = slice(128 * j, 128 * j + 128)
            k = k_V[(b, n)] = c_pe.up(three(PX[:, :], H[b % 2][:, c], L[b % 2][:, c], wvh[:, r], wvl[:, r]))
            wait(act, k, k_PV.get(8 * (b - 2) + 7))
            k_psx[0] = V[(b, n)] = c_act.up(act.copy(a_v[b % 2][:, j, r], PX[:, :]))

        def T(u):
            b, c = divmod(u, 8)
            wait(pe, *xT[b], *w_ready, k_tL.get(u - 1))
            for hh in range(2):
                h = 2 * c + hh
                r = slice(128 * h, 128 * h + 128)
                i = three(PT_[:, 256 * hh:256 * hh + 256], mh[:, r], ml[:, r], a_xth[b % 2][:, :], a_xtl[b % 2][:, :])
            k = k_T_[u] = c_pe.up(i)
            k_tH[u], k_tL[u] = split(a_th[u % 2][:, :], a_tl[u % 2][:, :], PT_[:, :], [k, k_S.get(u - 2)])

        def S(u):
            b, c = divmod(u, 8)
            H, L, marks = key(b)
            wait(pe, k_tH[u], k_tL[u], *marks[b])
            ring, mn, sm, rs = a_ring[u % 3], a_mn[u % 3], a_sm[u % 3], a_rs[u % 3]
            for hh in range(2):
                n = 2 * u + hh
                bank = PS[n % 3]
                wait(pe, k_mn.get(n - 3))
                for it in range(2):
                    w = 128 if causal and it == 0 else 256
                    q = slice(256 * hh + 128 * it, 256 * hh + 128 * it + 128)
                    i = three(bank[:, 256 * it:256 * it + w], a_th[u % 2][:, q], a_tl[u % 2][:, q],
                              H[b % 2][:, 0:w], L[b % 2][:, 0:w])
                k = c_pe.up(i)
                wait(dve, k, k_TR.get(2 * (u - 3) + hh), table_ready)
                for it in range(2):
                    w = 128 if causal and it == 0 else 256
                    k2 = c_dve.up(dve.tensor_tensor_reduce(
                        ring[:, hh, it, 0:w], bank[:, 256 * it:256 * it + w], table(2 * c + hh, it), 1.0, BIG,
                        ALU.add, ALU.min, mn[:, 2 * hh + it:2 * hh + it + 1]))
                k_mn[n] = k2
                wait(act, k2, k_nrm.get(u - 3))
                for it in range(2):
                    w = 128 if causal and it == 0 else 256
                    q = slice(2 * hh + it, 2 * hh + it + 1)
                    k3 = c_act.up(act.activation(ring[:, hh, it, 0:w], ring[:, hh, it, 0:w], ACT.Exp,
                                                 bias=mn[:, q], scale=-1.0, accum_out=sm[:, q]))
            k_S[u] = k
            wait(dve, k3)
            k4 = c_dve.up(dve.reciprocal(rs[:, :], sm[:, :]))
            wait(pool, k4, k3)
            for hh in range(2):
                for it in range(2):
                    w = 128 if causal and it == 0 else 256
                    q = slice(2 * hh + it, 2 * hh + it + 1)
                    k5 = c_pool.up(pool.tensor_scalar(ring[:, hh, it, 0:w], ring[:, hh, it, 0:w], rs[:, q], 1.0,
                                                      ALU.mult, ALU.mult))
            k_nrm[u] = k5

        def TR(u):
            ring = a_ring[u % 3]
            wait(pe, k_nrm[u])
            for hh in range(2):
                n = 2 * u + hh
                bank = PP[hh]
                wait(pe, k_PT.get(n - 2))
                for jt in range(2):
                    for it in range(2):
                        if causal and jt > it:
                            continue
                        i = tr(bank[:, 256 * jt + 128 * it:256 * jt + 128 * it + 128],
                               ring[:, hh, it, 128 * jt:128 * jt + 128])
                k = k_TR[n] = c_pe.up(i)
                eng, cnt = (dve, c_dve) if hh else (act, c_act)
                wait(eng, k, k_PV.get(u - 2))
                cp = dve.tensor_copy if hh else act.copy
                if causal:
                    cp(a_pt[u % 2][:, hh, 0:256], bank[:, 0:256])
                    k_PT[n] = cnt.up(cp(a_pt[u % 2][:, hh, 384:512], bank[:, 384:512]))
                else:
                    k_PT[n] = cnt.up(cp(a_pt[u % 2][:, hh, :], bank[:, :]))

        def PV(u):
            b, c = divmod(u, 8)
            wait(pe, k_PT[2 * u], k_PT[2 * u + 1], V[(b, 3)], k_O.get(u - 1))
            for jt in range(2):
                lo = 128 if causal and jt == 1 else 0
                for hh in range(2):
                    i = pe.matmul(PO[64 * hh:64 * hh + 64, lo:256],
                                  a_v[b % 2][:, jt, 128 * c + 64 * hh:128 * c + 64 * hh + 64],
                                  a_pt[u % 2][:, hh, 256 * jt + lo:256 * jt + 256], start=(jt == 0), stop=(jt == 1))
            k = k_PV[u] = c_pe.up(i)
            wait(dve, k, k_out.get(b - 1))
            k_O[u] = c_dve.up(dve.tensor_copy(a_ot[:, c, :], PO[:, 0:256]))

        def out(b):
            wait(pe, k_O[8 * b + 7], k_psx[0], *w_ready)
            for j in range(2):
                for c in range(8):
                    i = pe.matmul(PX[:, 128 * j:128 * j + 128], a_ot[:, c, 128 * j:128 * j + 128], wo[:, c, :],
                                  start=(c == 0), stop=(c == 7))
            k = k_out[b] = c_pe.up(i)
            xx = x[:, 2 * b:2 * b + 2, :]
            wait(dve, k, k_x[b])
            k = k_psx[0] = c_dve.up(dve.tensor_tensor(xx, PX[:, 0:256].rearrange("p (a d) -> p a d", a=2), xx, ALU.add))
            k1 = norm(xx, a_ph[:, :, :], s2, m2, r2, [k, k_phfree[0]])
            k_post[b] = k1
            k2 = norm(a_ph[:, :, :], xn[:, 2 * b:2 * b + 2, :], s2, m2, r2, [k1], gain=True)
            k_xn.append(k2)

        k_phfree = [None]
        k_xn = []
        k_lg = []

        def post_b(b):
            wait(pe, k_post[b], k_psx[0])
            for j in range(2):
                i = tr(PX[:, 128 * j:128 * j + 128], a_ph[:, j, :])
            k = c_pe.up(i)
            wait(act, k, k_pT_free[0])
            k_psx[0] = k_pT[0] = c_act.up(act.copy(a_pT[:, :], PX[:, 0:256]))
            k_phfree[0] = k_xn[-1]
            k_phpe[0] = k

        k_pT_free, k_pT, k_phpe = [None], [None], [None]

        def post_c(b):
            wait(pe, k_pT[0], d_wr)
            for j in range(2):
                i = pe.matmul(PX[:, 8 * j:8 * j + 8], a_pT[:, 128 * j:128 * j + 128], wr[:, :], start=True, stop=True)
            k = k_pT_free[0] = c_pe.up(i)
            wait(dve, k, d_b)
            k_psx[0] = c_dve.up(dve.tensor_tensor(
                lg[:, 2 * b:2 * b + 2, :], PX[:, 0:16].rearrange("p (a e) -> p a e", a=2),
                brb[:, :].rearrange("p (a e) -> p a e", a=1).broadcast_to((128, 2, NE)), ALU.add))
            k_lg.append(k_psx[0])

        n_u = 8 * NB
        pre_a(0)
        pre_b(0)
        if stage_b:
            pre_c(0)
        for s in range(n_u + 12):
            b, c = divmod(s, 8)
            if s < n_u:
                T(s)
            if s < n_u and c < 4:
                values(b, c)
            if 1 <= s <= n_u:
                S(s - 1)
            if b + 1 < NB and c == 3:
                pre_a(b + 1)
            if b + 1 < NB and c == 5:
                pre_b(b + 1)
            if b + 1 < NB and c == 6 and stage_b:
                pre_c(b + 1)
            if 3 <= s < n_u + 3:
                TR(s - 3)
            if s >= 12 and (s - 12) % 8 == 0:
                out((s - 12) // 8)
            if 4 <= s < n_u + 4:
                PV(s - 4)
            if s >= 14 and (s - 14) % 8 == 0:
                post_b((s - 14) // 8)
            if s >= 15 and (s - 15) % 8 == 0:
                post_c((s - 15) // 8)
            extra(s)
        post_b(NB - 1) if n_u + 12 <= 8 * NB - 8 + 14 else None
        post_c(NB - 1) if n_u + 12 <= 8 * NB - 8 + 15 else None
        return k_xn, k_lg

    def experts(k_xn, k_lg, first, finish, fill):
        E3 = lambda a: a.rearrange("p (t e) -> p t e", e=1).broadcast_to((128, NT, NE))
        T3 = lambda a: a.rearrange("p (t e) -> p t e", t=1).broadcast_to((128, NT, NE))
        A, B, C, D, OH, IN, TOT, CUM = f_oh
        mx, sm, gate, mk, pos = f_s[0:5]

        def V(i):
            k = c_dve.up(i)
            wait(dve, k)
            return k

        wait(dve, *k_lg)
        L3 = lg[:, :, :]
        k0 = V(dve.tensor_reduce(mx[:, :], L3, AX, ALU.max))
        k1 = V(dve.tensor_tensor(A[:, :, :], L3, E3(mx[:, :]), ALU.subtract))
        wait(act, k1)
        k2 = c_act.up(act.activation(B[:, :, :], A[:, :, :], ACT.Exp))
        V(dve.tensor_tensor(C[:, :, :], L3, E3(mx[:, :]), ALU.is_ge))
        V(dve.tensor_tensor(D[:, :, :], C[:, :, :], T3(iota_e[:, :]), ALU.mult))
        V(dve.tensor_reduce(mk[:, :], D[:, :, :], AX, ALU.max))
        k_oh = V(dve.tensor_tensor(OH[:, :, :], D[:, :, :], E3(mk[:, :]), ALU.is_equal))
        wait(pe, k_oh, k_tri)
        ohf = OH[:, :, :].rearrange("p t e -> p (t e)")
        pe.matmul(ps[0][:, 0:128], tri[:, :], ohf, start=True, stop=True)
        k_c = c_pe.up(pe.matmul(ps[1][:, 0:128], ones[:, :], ohf, start=True, stop=True))
        wait(dve, k2)
        V(dve.tensor_reduce(sm[:, :], B[:, :, :], AX, ALU.add))
        k_gate = V(dve.reciprocal(gate[:, :], sm[:, :]))
        wait(dve, k_c)
        f3 = lambda a: a.rearrange("p (t e) -> p t e", e=NE)
        V(dve.tensor_copy(TOT[:, :, :], f3(ps[1][:, 0:128])))
        src, dst = TOT, CUM
        for d in (1, 2, 4, 8):
            dve.tensor_copy(dst[:, 0:d, :], src[:, 0:d, :])
            V(dve.tensor_tensor(dst[:, d:, :], src[:, d:, :], src[:, 0:NT - d, :], ALU.add))
            src, dst = dst, (A if d % 4 == 1 else (B if d == 2 else C))
        inc = src
        tot = f_e[0]
        V(dve.tensor_copy(tot[:, :], inc[:, NT - 1, :]))
        V(dve.tensor_tensor(f_k16[:, :, :], tot[:, :].rearrange("p (e k) -> p e k", k=1).broadcast_to((128, NE, 16)),
                            iota_k[:, :].rearrange("p (e k) -> p e k", e=1).broadcast_to((128, NE, 16)), ALU.is_gt))
        V(dve.tensor_reduce(f_e[1][:, :], f_k16[:, :, :], AX, ALU.add))
        a, o = f_e[1], [f_e[2], f_e[3], f_e[4]]
        for n, d in enumerate((1, 2, 4)):
            dve.tensor_copy(o[n][:, 0:d], a[:, 0:d])
            V(dve.tensor_tensor(o[n][:, d:], a[:, d:], a[:, 0:NE - d], ALU.add))
            a = o[n]
        V(dve.tensor_tensor(f_e[5][:, :], a[:, :], f_e[1][:, :], ALU.subtract))
        V(dve.tensor_scalar(f_e[5][:, :], f_e[5][:, :], 128.0, None, ALU.mult))
        V(dve.tensor_tensor(IN[:, :, :], inc[:, :, :], TOT[:, :, :], ALU.subtract))
        V(dve.tensor_tensor(IN[:, :, :], f3(ps[0][:, 0:128]), IN[:, :, :], ALU.add))
        V(dve.tensor_tensor(IN[:, :, :], IN[:, :, :], T3(f_e[5][:, :]), ALU.add))
        V(dve.tensor_tensor(IN[:, :, :], IN[:, :, :], OH[:, :, :], ALU.mult))
        V(dve.tensor_reduce(pos[:, :], IN[:, :, :], AX, ALU.add))
        k_pos = V(dve.tensor_copy(f_i[:, :], pos[:, :]))
        V(dve.tensor_tensor(f_g[:, :, :], iota_s[:, :].rearrange("p (s e) -> p s e", e=1).broadcast_to((128, NS, NE)),
                            a[:, :].rearrange("p (s e) -> p s e", s=1).broadcast_to((128, NS, NE)), ALU.is_ge))
        V(dve.tensor_reduce(f_ef[:, :], f_g[:, :, :], AX, ALU.add))
        V(dve.tensor_scalar(f_ef[:, :], f_ef[:, :], float(NE - 1), None, ALU.min))
        k_ei = V(dve.tensor_copy(f_ei[:, :], f_ef[:, :]))
        wait(dve, k_pid)
        k_sel = V(dve.tensor_scalar(f_sel[:, :], f_ef[:, :], pid[:, 0:1], None, ALU.is_equal))

        c_sc = dma_sem()
        wait(pool, k_pos, *k_xn, d_zero)
        for j in range(NT):
            d_sc = c_sc.up(pool.indirect_dma_start(
                xs_dram, bass.IndirectOffsetOnAxis(ap=f_i[:, j:j + 1].bitcast(mybir.dt.uint32), axis=0), xn[:, j, :], None))
        wait(sp, d_sc)
        groups = [(4 * g, min(4 * g + 4, NS)) for g in range(6)]
        xsv = xs_dram.rearrange("(s p) d -> p s d", p=128)
        ysv = ys_dram.rearrange("(s p) d -> p s d", p=128)
        d_xs = [load(f_xs[:, a0:a1, :], xsv[:, a0:a1, :]) for a0, a1 in groups]
        fill()

        k_x, k_h, k_th, k_y = {}, {}, {}, {}
        k_hm, k_xfree, k_ht, k_ym = {}, {}, {}, {}
        wait(pe, k_ei)

        def XT(g):
            a0, a1 = groups[g]
            bank = ps[g % 2]
            wait(pe, d_xs[g], k_x.get(g - 2, (None, k_gate))[1])
            for s in range(a0, a1):
                i = tr(bank[:, 128 * (s - a0):128 * (s - a0) + 128], f_xs[:, s, :])
            k = c_pe.up(i)
            n = 128 * (a1 - a0)
            k_x[g] = split(f_xth[g % 2][:, 0:n], f_xtl[g % 2][:, 0:n], bank[:, 0:n],
                           [k, k_hm.get(4 * (g - 2) + 3)])

        def H(s):
            g, j = divmod(s, 4)
            bank = ps[2 + s % 2]
            wait(pe, *k_x[g], k_h.get(s - 2), k_ff[0], k_sel)
            r = slice(128 * j, 128 * j + 128)
            e = pe.value_load(f_ei[0:1, s:s + 1], min_val=0, max_val=NE - 1)
            wh, wl = w1h[:, bass.ds(e * 512, 512)], w1l[:, bass.ds(e * 512, 512)]
            three(bank[:, :], f_xth[g % 2][:, r], f_xtl[g % 2][:, r], wh, wl, last=False)
            i = pe.matmul(bank[:, :], f_sel[:, s:s + 1].broadcast_to((128, 128)), b1s[:, :], start=False, stop=True)
            k = k_hm[s] = c_pe.up(i)
            wait(act, k, k_th.get(s - 2))
            k_h[s] = c_act.up(act.activation(f_h[s % 2][:, :], bank[:, :], ACT.Relu))

        def HT(s):
            bank = ps[4 + s % 2]
            wait(pe, k_h[s], k_ht.get(s - 2, (None, None))[1])
            for f in range(4):
                i = tr(bank[:, 128 * f:128 * f + 128], f_h[s % 2][:, 128 * f:128 * f + 128])
            k = k_th[s] = c_pe.up(i)
            k_ht[s] = split(f_hth[s % 2][:, :], f_htl[s % 2][:, :], bank[:, :], [k, k_ym.get(s - 2)])

        def Y(s):
            bank = ps[6 + s % 2]
            wait(pe, *k_ht[s], k_y.get(s - 2))
            e = pe.value_load(f_ei[0:1, s:s + 1], min_val=0, max_val=NE - 1)
            o = bank[:, 0:128]
            for f in range(4):
                r = slice(128 * f, 128 * f + 128)
                hh_, hl_ = f_hth[s % 2][:, r], f_htl[s % 2][:, r]
                three(o, hh_, hl_, w2h[:, bass.ds(e * 512 + 128 * f, 128)], w2l[:, bass.ds(e * 512 + 128 * f, 128)],
                      first=(f == 0), last=False)
            i = pe.matmul(o, f_sel[:, s:s + 1].broadcast_to((128, 128)), b2s[:, :], start=False, stop=True)
            k = k_ym[s] = c_pe.up(i)
            wait(dve, k)
            k_y[s] = c_dve.up(dve.tensor_copy(f_ys[:, s, :], o))

        d_ys = []
        XT(0)
        XT(1)
        for s in range(NS + 2):
            if s < NS:
                H(s)
            if s % 4 == 3 and s // 4 + 2 < 6:
                XT(s // 4 + 2)
            if 1 <= s <= NS:
                HT(s - 1)
            if s >= 2:
                Y(s - 2)
                for a0, a1 in groups:
                    if s - 2 == a1 - 1:
                        d_ys.append(load(ysv[:, a0:a1, :], f_ys[:, a0:a1, :], after=[k_y[s - 2]]))
        wait(pool, *d_ys)
        c_ga = dma_sem()
        got = f_xs
        marks = []
        for j in range(NT):
            d = c_ga.up(pool.indirect_dma_start(
                got[:, j, :], None, ys_dram, bass.IndirectOffsetOnAxis(ap=f_i[:, j:j + 1].bitcast(mybir.dt.uint32), axis=0)))
        wait(dve, d, k_gate)
        for j in range(NT):
            k = c_dve.up(dve.scalar_tensor_tensor(x[:, j, :], got[:, j, :], gate[:, j:j + 1], x[:, j, :],
                                                  ALU.mult, ALU.add))
            marks.append(k)
            finish(j, k)
        return marks

    def all_done():
        return [(c, c.n) for c in (c_pe, c_dve, c_act, c_pool) if c.n]

    def barrier():
        m = all_done()
        for eng in (pe, dve, act, pool, sp):
            wait(eng, *m)

    barrier()

    def extra_a(s):
        if s % 2 == 0 and s // 2 < 16:
            stage_chunk(s // 2)
        if s == 34:
            stage_bias(t["b1"], b1s, 512)
        if s == 40:
            stage_bias(t["b2"], b2s, 128)

    TA = a_T[:, :, :].rearrange("p a b -> p (a b)")

    def table_a(h, it):
        if it == 1:
            return TA[:, 256 * h:256 * h + 256]
        o = TA[:, 256 * h + 128:256 * h + 256]
        return bass.AP(o.tensor, o.offset, [list(o.ap[0]), [4096 - 256 * h - 128, 2], [1, 128]])

    k_xn, k_lg = attention(False, lambda b: d_x, k_weights, table_a, k_T, extra_a)
    barrier()

    d_bq = load(bq[:, :], t["w_q"])
    d_bu = load(bu[:, :], t["w_kv_up"])
    d_bd = load(bkd[:, :], t["w_kv_down"])
    d_bo = load(wo[:, :, :], t["w_out_b"].rearrange("(c p) n -> p c n", p=128))
    k_wb = [d_bo]

    def weights_b():
        n = 0
        for src, dst, d in ((bq, bqT, d_bq), (bu, bkT, d_bu)):
            for g in range(2):
                bank = ps[2 + n]
                n += 1
                wait(pe, d)
                for j in range(4):
                    i = tr(bank[:, 128 * j:128 * j + 128], src[:, 512 * g + 128 * j:512 * g + 128 * j + 128])
                k = c_pe.up(i)
                wait(act, k)
                k = c_act.up(act.copy(dst[:, 4 * g:4 * g + 4, :], bank[:, :].rearrange("p (a b) -> p a b", a=4)))
        wait(pe, k)
        k_wb.extend(products(bqT, bkT, ps[2:6]))
        k_wb.extend(split(wvh[:, :], wvl[:, :], bu[:, 1024:2048], [d_bu]))
        k_wb.extend(split(kdh[:, :], kdl[:, :], bkd[:, :], [d_bd]))
        wait(pe, *k_wb)

    experts(k_xn, k_lg, True, lambda j, k: None, weights_b)
    barrier()

    CM = a_T[:, 0, :]
    k = c_pool.up(pool.memset(CM, 0.0))
    wait(pool, k)
    k_cm = c_pool.up(pool.affine_select(out=CM, in_=CM, compare_op=ALU.is_ge, fill=MASKED, base=128,
                                        pattern=[[-1, 256]], channel_multiplier=1))
    k_xn, k_lg = attention(True, lambda b: None, k_wb,
                           lambda h, it: CM if it == 1 else CM[:, 128:256], k_cm, lambda s: None)
    barrier()
    c_o = dma_sem()
    last = []

    def finish(j, k):
        if j % 4 == 3:
            last.append(load(ov[:, j - 3:j + 1, :], x[:, j - 3:j + 1, :], after=[k], c=c_o))

    experts(k_xn, k_lg, False, finish, lambda: None)
    wait(sp, last[-1])
    ctx.close()


_INS = ["L0_attn_a_x", "L0_attn_a_w_qkv", "L0_attn_a_w_out", "L0_attn_b_w_kv_down", "L0_attn_b_w_kv_up",
        "L0_attn_b_w_q", "L0_attn_b_w_out", "L0_ffn_Wr", "L0_ffn_br", "L0_ffn_ln_g", "L0_ffn_ln_b",
        "L0_ffn_W1", "L0_ffn_b1", "L0_ffn_W2", "L0_ffn_b2"]
_SHORT = {"L0_attn_a_x": "x", "L0_attn_a_w_qkv": "w_qkv", "L0_attn_a_w_out": "w_out_a",
          "L0_attn_b_w_kv_down": "w_kv_down", "L0_attn_b_w_kv_up": "w_kv_up", "L0_attn_b_w_q": "w_q",
          "L0_attn_b_w_out": "w_out_b", "L0_ffn_Wr": "Wr", "L0_ffn_br": "br", "L0_ffn_ln_g": "ln_g",
          "L0_ffn_ln_b": "ln_b", "L0_ffn_W1": "W1", "L0_ffn_b1": "b1", "L0_ffn_W2": "W2", "L0_ffn_b2": "b2"}


def kernel(**inputs):
    import concourse.bacc as bacc
    from concourse.bass_utils import run_bass_kernel_spmd

    nc = bacc.Bacc("TRN2", target_bir_lowering=False, num_devices=1)
    arrays, t = {}, {}

    def give(name, a):
        arrays[f"in_{name}"] = a
        t[name] = nc.dram_tensor(f"in_{name}", a.shape, mybir.dt.from_np(a.dtype), kind="ExternalInput").ap()

    for name in _INS:
        a = np.ascontiguousarray(inputs[name])
        give(_SHORT[name], a)
    rel = np.ascontiguousarray(inputs["L0_attn_a_rel_bias"])
    index = np.minimum(127 + np.arange(256)[None, :] - np.arange(128)[:, None], 254)
    give("bias", np.ascontiguousarray(rel[index].transpose(0, 2, 1)))
    t["out"] = nc.dram_tensor("out_0", (8, 256, 128), F32, kind="ExternalOutput").ap()
    build(nc, t)
    r = run_bass_kernel_spmd(nc, [arrays], core_ids=[0])
    return r.results[0]["out_0"]
```

```python
from contextlib import ExitStack

import numpy as np

import concourse.bass as bass
from concourse import mybir

F32 = mybir.dt.float32
F32R = mybir.dt.float32r
I32 = mybir.dt.int32
U32 = mybir.dt.uint32
ALU = mybir.AluOpType
ACT = mybir.ActivationFunctionType
AX = mybir.AxisListType.X

NT = 16
NB = 8
NC = 8
NE = 8
NS = 23
REG = 2048 + 128
XROWS = NE * REG + 7 * 128
NOWHERE = 1 << 20
EPS = 1e-5
BIG = 3.0e38
MASKED = 1.0e30


class Counter:

    def __init__(self, handle, step=1):
        self.handle, self.step, self.n = handle, step, 0

    def up(self, ins):
        ins.then_inc(self.handle, self.step)
        self.n += self.step
        return self, self.n


class Waits:

    def __init__(self):
        self.seen = {}

    def __call__(self, eng, *marks):
        for m in marks:
            if m is None:
                continue
            c, v = m
            key = (eng.engine, c)
            if self.seen.get(key, 0) < v:
                eng.wait_ge(c.handle, v)
                self.seen[key] = v


def build(nc, t):
    pe, dve, act, pool, sp = nc.tensor, nc.vector, nc.scalar, nc.gpsimd, nc.sync
    ctx = ExitStack()
    names = [0]

    def sem(name, step=1):
        return Counter(ctx.enter_context(nc.semaphore(name)), step)

    wait = Waits()
    c_pe, c_dve, c_act, c_pool = sem("c_pe"), sem("c_dve"), sem("c_act"), sem("c_pool")

    def sb(name, shape, dt=F32, scope=None):
        return (scope or ctx).enter_context(nc.sbuf_tensor(name, shape, dt))

    def dma_sem():
        names[0] += 1
        return sem(f"d{names[0]}", 16)

    class Spare:

        def __init__(self):
            self.free, self.n = {3: None, 7: None}, 3

        def take(self):
            self.n = 10 - self.n
            wait(pe, self.free[self.n])
            return ps[self.n], self.n

    spare = Spare()

    def load(dst, src, eng=None, after=(), c=None):
        eng = eng or sp
        wait(eng, *after)
        c = c or dma_sem()
        return c.up(eng.dma_start(dst, src))

    ps = [ctx.enter_context(nc.psum_tensor(f"ps{i}", [128, 512], F32)) for i in range(8)]
    PT_ = ps[0]
    PS = ps[1:3]
    PP = ps[4:6]
    PO = ps[6]

    xs_dram = nc.dram_tensor("xs_scratch", (XROWS, 129), F32).ap()
    ys_dram = nc.dram_tensor("ys_scratch", (NT * 128, 128), F32).ap()
    c_sc, c_ys, c_pad = dma_sem(), dma_sem(), dma_sem()
    d_row = [None]

    x = sb("x", [128, NT, 128])
    w1h, w1l = sb("w1h", [128, NE * 512], F32R), sb("w1l", [128, NE * 512], F32R)
    w2 = sb("w2", [128, NE * 4, 256], F32R)
    b1s = sb("b1s", [128, 512], F32R)
    b2s = sb("b2s", [128, 128], F32R)
    pid = sb("pid", [128, 1])
    pidi = sb("pidi", [128, 1], I32)
    xn = sb("xn", [128, NT, 129])
    gate = sb("gate", [128, NT])
    posi = sb("posi", [128, NT], I32)
    posf = sb("posf", [128, 4])
    run, runi = sb("run", [128, NE]), sb("runi", [128, NE], I32)
    bas, hot = sb("bas", [128, 4, NE]), sb("hot", [128, 4, NE])
    gmx, cnt = sb("gmx", [128, 4]), sb("cnt", [128, 64])
    padt = sb("padt", [128, 129])
    mh, ml = sb("mh", [128, 16 * 128], F32R), sb("ml", [128, 16 * 128], F32R)
    wvh, wvl = sb("wvh", [128, 1024], F32R), sb("wvl", [128, 1024], F32R)
    wo = sb("wo", [128, 8, 256], F32R)
    ident = sb("ident", [128, 128])
    tri = sb("tri", [128, 128])
    ones = sb("ones", [128, 128])
    lng, lnb = sb("lng", [128, 128]), sb("lnb", [128, 128])
    brb = sb("brb", [128, NE])
    wr = sb("wr", [128, NE])
    half = sb("half", [128, 16])
    stats = sb("stats", [128, 2, 6])
    mv = sb("mv", [128, 2, 2])
    rstd = sb("rstd", [128, 2])
    kdh, kdl = sb("kdh", [128, 128], F32R), sb("kdl", [128, 128], F32R)
    lg = sb("lg", [128, NT, NE])

    iota_i = sb("iota_i", [128, 32], I32)
    iota_e = sb("iota_e", [128, NE])
    iota_k = sb("iota_k", [128, 16])
    iota_s = sb("iota_s", [128, NS])
    cT = sb("cT", [128, 16])

    base = ExitStack()
    a_ring = [sb(f"ring{i}", [128, 2, 2, 256], scope=base) for i in range(3)]
    a_pt = [sb(f"pt{i}", [128, 2, 512], scope=base) for i in range(2)]
    a_th = [sb(f"th{i}", [128, 512], F32R, scope=base) for i in range(2)]
    a_tl = [sb(f"tl{i}", [128, 512], F32R, scope=base) for i in range(2)]
    a_v = [sb(f"v{i}", [128, 2, 1024], scope=base) for i in range(2)]
    a_oh = sb("oh", [128, 8, 256], F32R, scope=base)
    a_ol = sb("ol", [128, 8, 256], F32R, scope=base)
    a_xh = sb("xh", [128, 2, 128], scope=base)
    a_ph = sb("ph", [128, 2, 128], scope=base)
    a_pT = sb("pT", [128, 256], scope=base)
    a_xth = [sb(f"xth{i}", [128, 256], F32R, scope=base) for i in range(2)]
    a_xtl = [sb(f"xtl{i}", [128, 256], F32R, scope=base) for i in range(2)]
    a_mn = [sb(f"mn{i}", [128, 4], scope=base) for i in range(3)]
    a_sm = [sb(f"sm{i}", [128, 4], scope=base) for i in range(3)]
    a_rs = [sb(f"rs{i}", [128, 4], scope=base) for i in range(3)]
    s2 = sb("s2", [128, 2, 6], scope=base)
    m2 = sb("m2", [128, 2, 2], scope=base)
    r2 = sb("r2", [128, 2], scope=base)
    b_only = ExitStack()
    a_lth = [sb(f"lth{i}", [128, 256], F32R, scope=b_only) for i in range(2)]
    a_ltl = [sb(f"ltl{i}", [128, 256], F32R, scope=b_only) for i in range(2)]
    b_cm = sb("cm", [128, 256], scope=b_only)
    b_only.close()
    a_TA = sb("T", [128, 16 * 256 + 128], scope=base)
    a_T = a_TA[:, 0:4096].rearrange("p (h n) -> p h n", h=16)
    stage = [sb("stage", [128, 512], scope=base)]
    base.close()

    pre = ExitStack()
    wqn = sb("wqn", [128, 8, 128], scope=pre)
    wkn = sb("wkn", [128, 8, 128], scope=pre)
    wvn = sb("wvn", [128, 8, 128], scope=pre)
    won = sb("won", [128, 1024], scope=pre)
    pre.close()

    fs = ExitStack()
    f_xs = sb("f_xs", [128, NS, 129], scope=fs)
    f_ys = sb("f_ys", [128, NS, 128], scope=fs)
    f_xth = [sb(f"f_xth{i}", [128, 512], F32R, scope=fs) for i in range(2)]
    f_xtl = [sb(f"f_xtl{i}", [128, 512], F32R, scope=fs) for i in range(2)]
    f_h = [sb(f"f_h{i}", [128, 512], scope=fs) for i in range(2)]
    f_hth = [sb(f"f_hth{i}", [128, 512], F32R, scope=fs) for i in range(3)]
    f_htl = [sb(f"f_htl{i}", [128, 512], F32R, scope=fs) for i in range(3)]
    f_e = [sb(f"f_e{i}", [128, NE], scope=fs) for i in range(6)]
    f_g, f_g2 = sb("f_g", [128, NS, NE], scope=fs), sb("f_g2", [128, NS, NE], scope=fs)
    f_k16 = sb("f_k16", [128, NE, 16], scope=fs)
    f_row, f_ri = sb("f_row", [128, NS], scope=fs), sb("f_ri", [128, NS], I32, scope=fs)
    f_ei = sb("f_ei", [128, NS], I32, scope=fs)
    f_sub = sb("f_sub", [128, NT, NE], scope=fs)
    f_ef = sb("f_ef", [128, NS], scope=fs)
    f_sel = sb("f_sel", [128, NS], F32R, scope=fs)
    bq = sb("bq", [128, 1024], scope=fs)
    bu = sb("bu", [128, 2048], scope=fs)
    bqT = sb("bqT", [128, 8, 128], scope=fs)
    bkT = sb("bkT", [128, 8, 128], scope=fs)
    bkd = sb("bkd", [128, 128], scope=fs)
    bo = sb("bo", [128, 8, 128], scope=fs)
    fs.close()


    xv = t["x"].rearrange("b (s p) d -> p (b s) d", p=128)
    ov = t["out"].rearrange("b (s p) d -> p (b s) d", p=128)
    d_x = load(x[:, :, :], xv)
    wq3 = t["w_qkv"].rearrange("(d c h) x -> c d h x", c=3, h=16)
    c_w = dma_sem()
    for j, w in enumerate((wqn, wkn, wvn)):
        for hh in range(2):
            d_w = load(w[64 * hh:64 * hh + 64, :, :], wq3[j, :, hh::2, :], c=c_w, eng=act if hh else sp)
    d_won = load(won[:, :], t["w_out_a"])
    d_T = load(a_T[:, 0:16, :], t["bias"], eng=act)
    d_wr = load(wr[:, :], t["Wr"])
    c_b = dma_sem()
    load(lng[:, :], t["ln_g"].rearrange("(a d) -> a d", a=1).broadcast_to((128, 128)), c=c_b)
    load(lnb[:, :], t["ln_b"].rearrange("(a d) -> a d", a=1).broadcast_to((128, 128)), c=c_b)
    d_b = load(brb[:, :], t["br"].rearrange("(a d) -> a d", a=1).broadcast_to((128, NE)), c=c_b)

    def setup(ins):
        k = c_pool.up(ins)
        wait(pool, k)
        return k

    setup(pool.memset(ident[:, :], 0.0))
    k_id = setup(pool.affine_select(out=ident[:, :], in_=ident[:, :], compare_op=ALU.not_equal, fill=1.0,
                                    base=0, pattern=[[-1, 128]], channel_multiplier=1))
    k_h = setup(pool.memset(half[:, :], -0.5))
    setup(pool.memset(ones[:, :], 1.0))
    k_tri = setup(pool.affine_select(out=tri[:, :], in_=ones[:, :], compare_op=ALU.is_gt, fill=0.0,
                                     base=0, pattern=[[1, 128]], channel_multiplier=-1))
    k_T0 = setup(pool.memset(a_TA[:, 4096:4224], 0.0))
    setup(pool.memset(b1s[:, :].bitcast(F32), 0.0))
    k_b0 = setup(pool.memset(b2s[:, :].bitcast(F32), 0.0))
    setup(pool.memset(pid[:, :], -1.0))
    for row in (0, 32):
        setup(pool.iota(pidi[row:row + NE, :], pattern=[[0, 1]], base=0, channel_multiplier=1))
        k_pid = setup(pool.tensor_copy(pid[row:row + NE, :], pidi[row:row + NE, :]))
    setup(pool.iota(iota_i[:, :], pattern=[[1, 32]], base=0, channel_multiplier=0))
    setup(pool.tensor_copy(iota_s[:, :], iota_i[:, 0:NS]))
    setup(pool.tensor_scalar(iota_k[:, :], iota_i[:, 0:16], 128.0, 0.0, ALU.mult, ALU.add))
    k_iota = setup(pool.tensor_scalar(iota_e[:, :], iota_i[:, 0:NE], -1.0, float(NE), ALU.mult, ALU.add))
    setup(pool.memset(padt[:, 0:128], 0.0))
    k_padt = setup(pool.memset(padt[:, 128:129].bitcast(I32), NOWHERE))
    k_tok = setup(pool.iota(xn[:, :, 128:129].bitcast(I32).rearrange("p t a -> p (t a)"), pattern=[[128, NT]], base=0,
                            channel_multiplier=1))
    d_empty = load(xs_dram[NE * REG:XROWS, :].rearrange("(k p) d -> p k d", p=128),
                   padt[:, :].rearrange("p (k d) -> p k d", k=1).broadcast_to((128, 7, 129)), after=[k_padt])

    def split(high, low, src, after, scale=None, he=act, le=dve):
        wait(he, *after)
        cnt = {id(act): c_act, id(dve): c_dve, id(pool): c_pool}
        if he is act:
            i = act.activation(high, src, ACT.Copy, scale=1.0 if scale is None else scale)
        else:
            i = he.tensor_copy(high, src)
        a = cnt[id(he)].up(i)
        wait(le, a, *after)
        if scale is None:
            i = le.tensor_tensor(low, src, high.bitcast(F32), ALU.subtract)
        else:
            i = le.scalar_tensor_tensor(low, src, scale, high.bitcast(F32), ALU.mult, ALU.subtract)
        return a, cnt[id(le)].up(i)

    def three(out, ah, al, bh, bl, first=True, last=True):
        pe.matmul(out, ah, bh, start=first, stop=False)
        pe.matmul(out, al, bh, start=False, stop=False)
        return pe.matmul(out, ah, bl, start=False, stop=last)

    def tr(out, src):
        return pe.transpose(out, src, ident[:, :])

    def products(q, k, banks):
        marks = []
        for g in range(2):
            for hh in range(2):
                bank = banks[2 * g + hh]
                rows = slice(64 * hh, 64 * hh + 64)
                for j in range(4):
                    i = pe.matmul(bank[:, 128 * j:128 * j + 128], q[rows, 4 * g + j, :], k[rows, 4 * g + j, :],
                                  start=True, stop=True)
                m = c_pe.up(i)
                v = [w[:, :].rearrange("p (c h n) -> p h c n", h=2, n=128)[:, hh, 4 * g:4 * g + 4, :] for w in (mh, ml)]
                marks += split(*v, bank[:, :].rearrange("p (c n) -> p c n", c=4), [m], scale=-0.125)
        return marks

    free = [None] * 8
    wait(pe, d_w, k_id)
    k_m = []
    k_m += products(wqn, wkn, ps[0:4])
    for g in range(2):
        bank = ps[4 + g]
        for j in range(4):
            i = tr(bank[:, 128 * j:128 * j + 128], wvn[:, 4 * g + j, :])
        k = c_pe.up(i)
        r = slice(512 * g, 512 * g + 512)
        k_m += split(wvh[:, r], wvl[:, r], bank[:, :], [k])
    wait(pe, d_won)
    for g in range(2):
        bank = ps[6 + g]
        for j in range(4):
            i = tr(bank[:, 128 * j:128 * j + 128], won[:, 512 * g + 128 * j:512 * g + 128 * j + 128])
        k = c_pe.up(i)
        w = wo[:, 4 * g:4 * g + 4, :]
        k_m += split(w[:, :, 0:128], w[:, :, 128:256], bank[:, :].rearrange("p (c n) -> p c n", c=4), [k])
    wait(pool, d_T, k_T0)
    tc = a_T[:, 0:16, 255:256]
    wait(dve, d_T)
    k = c_dve.up(dve.tensor_copy(cT[:, :], tc.rearrange("p a b -> p (a b)")))
    wait(dve, k)
    k_T = c_dve.up(dve.tensor_tensor(a_T[:, 0:16, :], cT[:, :].rearrange("p (a b) -> p a b", b=1).broadcast_to((128, 16, 256)),
                                     a_T[:, 0:16, :], ALU.subtract))
    k_weights = k_m + [k_T, k_T0]

    stage_free = [None]
    chunks = []
    for e in range(NE):
        r = slice(512 * e, 512 * e + 512)
        chunks.append((w1h[:, r], w1l[:, r], t["W1"][e]))
        w = w2[:, 4 * e:4 * e + 4, :]
        chunks.append((w[:, :, 0:128], w[:, :, 128:256], t["W2"][e].rearrange("(c p) d -> p c d", p=128)))
    c_st = [dma_sem()]
    k_high = [None]
    k_ff, k_fb = [None], [None]

    def stage_load(n):
        s = stage[0]
        h, l, src = chunks[n]
        dst = s[:, :] if len(src.shape) == 2 else s[:, :].rearrange("p (c d) -> p c d", c=4)
        d_stage[n] = load(dst, src, after=[stage_free[0]], c=c_st[0])

    def stage_split(n):
        s = stage[0]
        h, l, src = chunks[n]
        v = s[:, :] if len(src.shape) == 2 else s[:, :].rearrange("p (c d) -> p c d", c=4)
        wait(act, d_stage[n])
        k_high[0] = c_act.up(act.copy(h, v))

    def stage_low(n):
        s = stage[0]
        h, l, src = chunks[n]
        v = s[:, :] if len(src.shape) == 2 else s[:, :].rearrange("p (c d) -> p c d", c=4)
        wait(dve, k_high[0], d_stage[n])
        stage_free[0] = c_dve.up(dve.tensor_tensor(l, v, h.bitcast(F32), ALU.subtract))
        k_ff[0] = stage_free[0]

    d_stage = {}

    def stage_bias(src, dst, w):
        s, c = stage[0], c_st[0]
        for row in (0, 32):
            d = load(s[row:row + NE, 0:w], src, after=[stage_free[0]], c=c)
        wait(dve, d, k_b0)
        for row in (0, 32):
            k = c_dve.up(dve.tensor_copy(dst[row:row + NE, :], s[row:row + NE, 0:w]))
        wait(dve, k)
        stage_free[0] = k_fb[0] = c_dve.up(dve.tensor_tensor(
            dst[32:32 + NE, :], s[32:32 + NE, 0:w], dst[32:32 + NE, :].bitcast(F32), ALU.subtract))

    def norm_a(src, st, m, r, after):
        wait(dve, *after)
        for j in range(2):
            k = c_dve.up(dve.bn_stats(st[:, j, :], src[:, j, :]))
        wait(dve, k)
        for j in range(2):
            k = c_dve.up(dve.bn_aggr(m[:, j, :], st[:, j, :]))
        wait(dve, k)
        k = c_dve.up(dve.tensor_scalar(r[:, :], m[:, :, 1], EPS, None, ALU.add))
        wait(pool, k, k_h)
        return c_pool.up(pool.tensor_tensor(r[:, :], r[:, :], half[:, 0:2], ALU.pow))

    def norm_b(dst, src, m, r, k, *after):
        wait(dve, k, *after)
        for j in range(2):
            k = c_dve.up(dve.tensor_scalar(dst[:, j, :], src[:, j, :], m[:, j, 0:1], r[:, j:j + 1],
                                           ALU.subtract, ALU.mult))
        return k

    def gain(dst, k):
        wait(pool, k, d_b)
        bc = lambda a: a[:, :].rearrange("p (a d) -> p a d", a=1).broadcast_to((128, 2, 128))
        k = c_pool.up(pool.tensor_tensor(dst, dst, bc(lng), ALU.mult))
        wait(pool, k)
        return c_pool.up(pool.tensor_tensor(dst, dst, bc(lnb), ALU.add))

    def attention(stage_b, x_ready, w_ready, table, table_ready, extra):
        causal = stage_b
        xT, lT, V = {}, {}, {}
        k_T_, k_tH, k_tL, k_S, k_mn, k_exp, k_nrm, k_TR, k_PT, k_PV, k_O, k_OH = ({} for _ in range(12))
        k_out, k_xh_free, k_post = {}, [None], {}
        k_x = {}
        last_T = {}

        k_r1 = {}

        def pre_a(b):
            k_r1[b] = norm_a(x[:, 2 * b:2 * b + 2, :], stats, mv, rstd, [x_ready(b), k_x.get(b - 1)])

        def pre_a2(b):
            k_x[b] = norm_b(a_xh, x[:, 2 * b:2 * b + 2, :], mv, rstd, k_r1[b], k_xh_free[0])

        def pre_b(b):
            PX, n = spare.take()
            wait(pe, k_x[b], k_id)
            for j in range(2):
                i = tr(PX[:, 128 * j:128 * j + 128], a_xh[:, j, :])
            k = c_pe.up(i)
            k_xh_free[0] = k
            gone = ([k_lat.get(b - 2), k_T_.get(8 * (b - 2) + 7)] if stage_b
                    else [k_S.get(8 * (b - 2) + 7), k_V.get((b - 2, 3))])
            xT[b] = split(a_xth[b % 2][:, :], a_xtl[b % 2][:, :], PX[:, 0:256], [k, *gone])
            spare.free[n] = xT[b][1]

        k_lat = {}
        k_V = {}

        def pre_c(b):
            PX, n = spare.take()
            wait(pe, *xT[b], *w_ready)
            k = k_lat[b] = c_pe.up(three(PX[:, 0:256], kdh[:, :], kdl[:, :], a_xth[b % 2][:, :], a_xtl[b % 2][:, :]))
            lT[b] = split(a_lth[b % 2][:, :], a_ltl[b % 2][:, :], PX[:, 0:256],
                          [k, k_S.get(8 * (b - 2) + 7), k_V.get((b - 2, 3))])
            spare.free[n] = lT[b][1]

        def key(b):
            return (a_lth, a_ltl, lT) if stage_b else (a_xth, a_xtl, xT)

        def values(b, n):
            H, L, marks = key(b)
            j, half_ = n // 2, n % 2
            PX, m = spare.take()
            wait(pe, *marks[b], *w_ready)
            r = slice(512 * half_, 512 * half_ + 512)
            c = slice(128 * j, 128 * j + 128)
            k = k_V[(b, n)] = c_pe.up(three(PX[:, :], H[b % 2][:, c], L[b % 2][:, c], wvh[:, r], wvl[:, r]))
            wait(act, k, k_PV.get(8 * (b - 2) + 7))
            spare.free[m] = V[(b, n)] = c_act.up(act.copy(a_v[b % 2][:, j, r], PX[:, :]))

        def T(u):
            b, c = divmod(u, 8)
            wait(pe, *xT[b], *w_ready, k_tL.get(u - 1))
            for hh in range(2):
                h = 2 * c + hh
                r = slice(128 * h, 128 * h + 128)
                i = three(PT_[:, 256 * hh:256 * hh + 256], mh[:, r], ml[:, r], a_xth[b % 2][:, :], a_xtl[b % 2][:, :])
            k = k_T_[u] = c_pe.up(i)
            k_tH[u], k_tL[u] = split(a_th[u % 2][:, :], a_tl[u % 2][:, :], PT_[:, :], [k, k_S.get(u - 2)])

        def S(u):
            b, c = divmod(u, 8)
            H, L, marks = key(b)
            wait(pe, k_tH[u], k_tL[u], *marks[b])
            ring, mn, sm, rs = a_ring[u % 3], a_mn[u % 3], a_sm[u % 3], a_rs[u % 3]
            for hh in range(2):
                n = 2 * u + hh
                bank = PS[n % 2]
                wait(pe, k_mn.get(n - 2))
                for it in range(2):
                    w = 128 if causal and it == 0 else 256
                    q = slice(256 * hh + 128 * it, 256 * hh + 128 * it + 128)
                    i = three(bank[:, 256 * it:256 * it + w], a_th[u % 2][:, q], a_tl[u % 2][:, q],
                              H[b % 2][:, 0:w], L[b % 2][:, 0:w])
                k = c_pe.up(i)
                wait(dve, k, k_TR.get(2 * (u - 3) + hh), table_ready)
                for it in range(2):
                    w = 128 if causal and it == 0 else 256
                    k2 = c_dve.up(dve.tensor_tensor_reduce(
                        ring[:, hh, it, 0:w], bank[:, 256 * it:256 * it + w], table(2 * c + hh, it), 1.0, BIG,
                        ALU.add, ALU.min, mn[:, 2 * hh + it:2 * hh + it + 1]))
                k_mn[n] = k2
            k_S[u] = k

        def expo(u):
            ring, mn, sm = a_ring[u % 3], a_mn[u % 3], a_sm[u % 3]
            for hh in range(2):
                wait(act, k_mn[2 * u + hh], *k_nrm.get(u - 3, ()))
                for it in range(2):
                    w = 128 if causal and it == 0 else 256
                    q = slice(2 * hh + it, 2 * hh + it + 1)
                    k3 = c_act.up(act.activation(ring[:, hh, it, 0:w], ring[:, hh, it, 0:w], ACT.Exp,
                                                 bias=mn[:, q], scale=-1.0, accum_out=sm[:, q]))
            k_exp[u] = k3

        def weigh(u):
            ring, sm, rs = a_ring[u % 3], a_sm[u % 3], a_rs[u % 3]
            k3 = k_exp[u]
            wait(dve, k3)
            k4 = c_dve.up(dve.reciprocal(rs[:, :], sm[:, :]))
            wait(pool, k4, k3)
            wait(dve, k4)
            k5 = {}
            for hh in range(2):
                for it in range(2):
                    w = 128 if causal and it == 0 else 256
                    q = slice(2 * hh + it, 2 * hh + it + 1)
                    eng, cnt = (pool, c_pool)
                    k5[cnt] = cnt.up(eng.tensor_scalar(ring[:, hh, it, 0:w], ring[:, hh, it, 0:w], rs[:, q], 1.0,
                                                       ALU.mult, ALU.mult))
            k_nrm[u] = list(k5.values())

        def TR(u):
            ring = a_ring[u % 3]
            wait(pe, *k_nrm[u])
            for hh in range(2):
                n = 2 * u + hh
                bank = PP[hh]
                wait(pe, k_PT.get(n - 2))
                for jt in range(2):
                    for it in range(2):
                        if causal and jt > it:
                            continue
                        i = tr(bank[:, 256 * jt + 128 * it:256 * jt + 128 * it + 128],
                               ring[:, hh, it, 128 * jt:128 * jt + 128])
                k = k_TR[n] = c_pe.up(i)
                eng, cnt = (dve, c_dve) if hh else (act, c_act)
                wait(eng, k, k_PV.get(u - 2))
                cp = dve.tensor_copy if hh else act.copy
                if causal:
                    cp(a_pt[u % 2][:, hh, 0:256], bank[:, 0:256])
                    k_PT[n] = cnt.up(cp(a_pt[u % 2][:, hh, 384:512], bank[:, 384:512]))
                else:
                    k_PT[n] = cnt.up(cp(a_pt[u % 2][:, hh, :], bank[:, :]))

        def PV(u):
            b, c = divmod(u, 8)
            wait(pe, k_PT[2 * u], k_PT[2 * u + 1], V[(b, 3)], k_O.get(u - 1))
            for jt in range(2):
                lo = 128 if causal and jt == 1 else 0
                for hh in range(2):
                    i = pe.matmul(PO[64 * hh:64 * hh + 64, lo:256],
                                  a_v[b % 2][:, jt, 128 * c + 64 * hh:128 * c + 64 * hh + 64],
                                  a_pt[u % 2][:, hh, 256 * jt + lo:256 * jt + 256], start=(jt == 0), stop=(jt == 1))
            k_PV[u] = c_pe.up(i)

        def keep(u):
            b, c = divmod(u, 8)
            k_OH[u], k_O[u] = split(a_oh[:, c, :], a_ol[:, c, :], PO[:, 0:256], [k_PV[u], k_out.get(b - 1)])

        def out(b):
            PX, n = spare.take()
            wait(pe, k_O[8 * b + 7], k_OH[8 * b + 7], *w_ready)
            for j in range(2):
                for c in range(8):
                    r = slice(128 * j, 128 * j + 128)
                    pe.matmul(PX[:, 256 * j:256 * j + 256], a_oh[:, c, r], wo[:, c, :], start=(c == 0), stop=False)
                    i = pe.matmul(PX[:, 256 * j:256 * j + 128], a_ol[:, c, r], wo[:, c, 0:128],
                                  start=False, stop=(c == 7))
            k = k_out[b] = c_pe.up(i)
            xx = x[:, 2 * b:2 * b + 2, :]
            px = PX[:, :].rearrange("p (a h d) -> p h a d", a=2, h=2)
            wait(dve, k, k_x[b])
            for h in range(2):
                k = spare.free[n] = c_dve.up(dve.tensor_tensor(xx, px[:, h, :, :], xx, ALU.add))
                wait(dve, k)
            k_post[b] = norm_a(xx, s2, m2, r2, [k])

        def post_a(b):
            k = k_post[b] = norm_b(a_ph, x[:, 2 * b:2 * b + 2, :], m2, r2, k_post[b], k_phpe[0], k_phdve[0])
            k_lg2[b] = norm_a(a_ph, s2, m2, r2, [k])

        def post_a2(b):
            xx = xn[:, 2 * b:2 * b + 2, 0:128]
            k = k_phdve[0] = norm_b(xx, a_ph, m2, r2, k_lg2[b])
            k_xn[b] = gain(xx, k)

        k_lg2, k_xn, k_hot, k_pre = {}, {}, {}, {}
        k_phdve, k_pT_free, k_pT, k_phpe = [None], [None], [None], [None]

        def post_b(b):
            PX, n = spare.take()
            wait(pe, k_post[b])
            for j in range(2):
                i = tr(PX[:, 128 * j:128 * j + 128], a_ph[:, j, :])
            k = k_phpe[0] = c_pe.up(i)
            wait(act, k, k_pT_free[0])
            spare.free[n] = k_pT[0] = c_act.up(act.copy(a_pT[:, :], PX[:, 0:256]))

        def post_c(b):
            PX, n = spare.take()
            wait(pe, k_pT[0], d_wr)
            for j in range(2):
                i = pe.matmul(PX[:, 8 * j:8 * j + 8], a_pT[:, 128 * j:128 * j + 128], wr[:, :], start=True, stop=True)
            k = k_pT_free[0] = c_pe.up(i)
            wait(dve, k, d_b, k_iota)
            k = spare.free[n] = c_dve.up(dve.tensor_tensor(
                lg[:, 2 * b:2 * b + 2, :], PX[:, 0:16].rearrange("p (t e) -> p t e", t=2),
                brb[:, :].rearrange("p (t e) -> p t e", t=1).broadcast_to((128, 2, NE)), ALU.add))
            if b in ROUTED:
                wait(dve, k)
                k_hot[b] = choose(*ROUTED[b])

        def post_d(b):
            if b not in ROUTED:
                return
            t0, t1 = ROUTED[b]
            n8 = 8 * (t1 - t0)
            PX, n = spare.take()
            wait(pe, k_hot[b], k_tri)
            h = hot[:, 0:t1 - t0, :].rearrange("p t e -> p (t e)")
            pe.matmul(PX[:, 0:n8], tri[:, :], h, start=True, stop=True)
            k = c_pe.up(pe.matmul(PX[:, n8:2 * n8], ones[:, :], h, start=True, stop=True))
            wait(act, k, k_cnt_free[0])
            spare.free[n] = k_cnt[b] = c_act.up(act.copy(cnt[:, 0:2 * n8], PX[:, 0:2 * n8]))

        k_cnt, k_cnt_free = {}, [None]

        def post_e(b):
            if b in ROUTED:
                k_cnt_free[0], d_row[0] = place(*ROUTED[b], k_cnt[b], k_xn[b])

        n_u = 8 * NB
        POST = ((14, post_a), (15, post_a2), (15, post_b), (16, post_c), (17, post_d), (18, post_e))

        def at(s, lag):
            b, c = divmod(s - lag, 8)
            return b if c == 0 and 0 <= b < NB else None

        pre_a(0)
        pre_a2(0)
        pre_b(0)
        if stage_b:
            pre_c(0)
        for s in range(n_u + 12):
            if 5 <= s < n_u + 5:
                keep(s - 5)
            if s < n_u:
                T(s)
            if 4 <= s < n_u + 4:
                TR(s - 4)
            if s < n_u and s % 8 < 4:
                values(*divmod(s, 8))
            if 3 <= s < n_u + 3:
                weigh(s - 3)
            if 2 <= s < n_u + 2:
                expo(s - 2)
            if 1 <= s <= n_u:
                S(s - 1)
            for lag, what in ((-6, pre_a), (-5, pre_a2), (-3, pre_b), (-2, pre_c if stage_b else None)):
                b = at(s, lag)
                if b and what:
                    what(b)
            if (b := at(s, 12)) is not None:
                out(b)
            if 4 <= s < n_u + 4:
                PV(s - 4)
            for lag, what in POST:
                if (b := at(s, lag)) is not None:
                    what(b)
            extra(s)

    def V(i):
        k = c_dve.up(i)
        wait(dve, k)
        return k

    def start_rows():
        V(dve.tensor_scalar(run[:, :], iota_s[:, 0:NE], float(REG), None, ALU.mult))

    ROUTED = {1: (0, 4), 3: (4, 8), 5: (8, 12), 6: (12, 14), 7: (14, 16)}

    def by_tile(a, n):
        return a.rearrange("p (t e) -> p t e", e=1).broadcast_to((128, n, NE))

    def by_expert(a, n):
        return a.rearrange("p (t e) -> p t e", t=1).broadcast_to((128, n, NE))

    def choose(t0, t1):
        n = t1 - t0
        l, h, g = lg[:, t0:t1, :], hot[:, 0:n, :], gmx[:, 0:n]
        V(dve.tensor_reduce(g, l, AX, ALU.max))
        V(dve.tensor_tensor(h, l, by_tile(g, n), ALU.is_ge))
        V(dve.tensor_tensor(h, h, by_expert(iota_e[:, :], n), ALU.mult))
        V(dve.tensor_reduce(g, h, AX, ALU.max))
        return V(dve.tensor_tensor(h, h, by_tile(g, n), ALU.is_equal))

    def place(t0, t1, k, k_rows):
        n = t1 - t0
        c = cnt[:, 0:16 * n].rearrange("p (a t e) -> p a t e", a=2, e=NE)
        wait(dve, k)
        V(dve.tensor_copy(bas[:, 0, :], run[:, :]))
        for j in range(1, n + 1):
            V(dve.tensor_tensor(bas[:, j, :] if j < n else run[:, :], c[:, 1, j - 1, :], bas[:, j - 1, :], ALU.add))
        b = bas[:, 0:n, :]
        k0 = V(dve.tensor_tensor(b, c[:, 0, :, :], b, ALU.add))
        V(dve.tensor_tensor(b, b, hot[:, 0:n, :], ALU.mult))
        V(dve.tensor_reduce(posf[:, 0:n], b, AX, ALU.add))
        k1 = V(dve.tensor_copy(posi[:, t0:t1], posf[:, 0:n]))
        wait(pool, k1, k_rows, k_tok)
        for j in range(t0, t1):
            d = c_sc.up(pool.indirect_dma_start(
                xs_dram, bass.IndirectOffsetOnAxis(ap=posi[:, j:j + 1].bitcast(U32), axis=0), xn[:, j, :], None))
        return k0, d

    def gates():
        E3 = lambda a: by_tile(a, NT)
        V(dve.tensor_reduce(gate[:, :], lg[:, :, :], AX, ALU.max))
        k = V(dve.tensor_tensor(f_sub[:, :, :], lg[:, :, :], E3(gate[:, :]), ALU.subtract))
        wait(act, k)
        k = c_act.up(act.activation(f_sub[:, :, :], f_sub[:, :, :], ACT.Exp))
        wait(dve, k)
        V(dve.tensor_reduce(gate[:, :], f_sub[:, :, :], AX, ALU.add))
        V(dve.reciprocal(gate[:, :], gate[:, :]))

    def experts(finish, fill):
        V(dve.tensor_copy(runi[:, :], run[:, :]))
        k_run = (c_dve, c_dve.n)
        for e in range(NE):
            wait(act, k_run, k_padt)
            r = act.value_load(runi[0:1, e:e + 1], min_val=0, max_val=NE * REG)
            d_pad = c_pad.up(act.dma_start(xs_dram[bass.ds(r, 128), :], padt[:, :]))
        tot = f_e[0]
        V(dve.scalar_tensor_tensor(tot[:, :], iota_s[:, 0:NE], -float(REG), run[:, :], ALU.mult, ALU.add))
        V(dve.tensor_tensor(f_k16[:, :, :], tot[:, :].rearrange("p (e k) -> p e k", k=1).broadcast_to((128, NE, 16)),
                            iota_k[:, :].rearrange("p (e k) -> p e k", e=1).broadcast_to((128, NE, 16)), ALU.is_gt))
        V(dve.tensor_reduce(f_e[1][:, :], f_k16[:, :, :], AX, ALU.add))
        a, o = f_e[1], [f_e[2], f_e[3], f_e[4]]
        for n, d in enumerate((1, 2, 4)):
            dve.tensor_copy(o[n][:, 0:d], a[:, 0:d])
            V(dve.tensor_tensor(o[n][:, d:], a[:, d:], a[:, 0:NE - d], ALU.add))
            a = o[n]
        V(dve.tensor_scalar(f_e[5][:, :], f_e[1][:, :], -128.0, float(REG), ALU.mult, ALU.add))
        V(dve.tensor_tensor(f_g[:, :, :], iota_s[:, :].rearrange("p (s e) -> p s e", e=1).broadcast_to((128, NS, NE)),
                            a[:, :].rearrange("p (s e) -> p s e", s=1).broadcast_to((128, NS, NE)), ALU.is_ge))
        V(dve.tensor_tensor(f_g2[:, :, :], f_g[:, :, :],
                            f_e[5][:, :].rearrange("p (s e) -> p s e", s=1).broadcast_to((128, NS, NE)), ALU.mult))
        V(dve.tensor_reduce(f_row[:, :], f_g2[:, :, :], AX, ALU.add))
        V(dve.scalar_tensor_tensor(f_row[:, :], iota_s[:, :], 128.0, f_row[:, :], ALU.mult, ALU.add))
        k_row = V(dve.tensor_copy(f_ri[:, :], f_row[:, :]))
        wait(sp, k_row, d_row[0], d_pad, d_empty)
        c_xs = [dma_sem() for _ in range(6)]
        groups = [(4 * g, min(4 * g + 4, NS)) for g in range(6)]
        d_xs = []
        for g, (a0, a1) in enumerate(groups):
            for s in range(a0, a1):
                r = sp.value_load(f_ri[0:1, s:s + 1], min_val=0, max_val=XROWS - 128)
                d = c_xs[g].up(sp.dma_start(f_xs[:, s, :], xs_dram[bass.ds(r, 128), :]))
            d_xs.append(d)
        V(dve.tensor_reduce(f_ef[:, :], f_g[:, :, :], AX, ALU.add))
        V(dve.tensor_scalar(f_ef[:, :], f_ef[:, :], float(NE - 1), None, ALU.min))
        k_ei = V(dve.tensor_copy(f_ei[:, :], f_ef[:, :]))
        wait(dve, k_pid)
        k_sel = V(dve.tensor_scalar(f_sel[:, :], f_ef[:, :], pid[:, 0:1], None, ALU.is_equal))
        fill()
        gates()

        k_x, k_h, k_th, k_y = {}, {}, {}, {}
        k_hm, k_xfree, k_ht, k_ym = {}, {}, {}, {}
        wait(pe, k_ei)

        def XT(g):
            a0, a1 = groups[g]
            bank = ps[g % 2]
            wait(pe, d_xs[g], k_x.get(g - 2, (None, k_ei))[1])
            for s in range(a0, a1):
                i = tr(bank[:, 128 * (s - a0):128 * (s - a0) + 128], f_xs[:, s, 0:128])
            k = c_pe.up(i)
            n = 128 * (a1 - a0)
            k_x[g] = split(f_xth[g % 2][:, 0:n], f_xtl[g % 2][:, 0:n], bank[:, 0:n],
                           [k, k_hm.get(4 * (g - 2) + 3)])

        def H(s):
            g, j = divmod(s, 4)
            bank = ps[2 + s % 2]
            wait(pe, *k_x[g], k_h.get(s - 2), k_ff[0], k_fb[0], k_sel)
            r = slice(128 * j, 128 * j + 128)
            e = pe.value_load(f_ei[0:1, s:s + 1], min_val=0, max_val=NE - 1)
            wh, wl = w1h[:, bass.ds(e * 512, 512)], w1l[:, bass.ds(e * 512, 512)]
            three(bank[:, :], f_xth[g % 2][:, r], f_xtl[g % 2][:, r], wh, wl, last=False)
            i = pe.matmul(bank[:, :], f_sel[:, s:s + 1].broadcast_to((128, 128)), b1s[:, :], start=False, stop=True)
            k = k_hm[s] = c_pe.up(i)
            wait(act, k, k_th.get(s - 2))
            k_h[s] = c_act.up(act.activation(f_h[s % 2][:, :], bank[:, :], ACT.Relu))

        def HT(s):
            bank = ps[4 + s % 2]
            wait(pe, k_h[s], k_ht.get(s - 2, (None, None))[1])
            for f in range(4):
                i = tr(bank[:, 128 * f:128 * f + 128], f_h[s % 2][:, 128 * f:128 * f + 128])
            k = k_th[s] = c_pe.up(i)
            k_ht[s] = split(f_hth[s % 3][:, :], f_htl[s % 3][:, :], bank[:, :], [k, k_ym.get(s - 3)])

        def Y(s):
            bank = ps[6 + s % 2]
            wait(pe, *k_ht[s], k_y.get(s - 2))
            e = pe.value_load(f_ei[0:1, s:s + 1], min_val=0, max_val=NE - 1)
            o = bank[:, 0:128]
            for f in range(4):
                r = slice(128 * f, 128 * f + 128)
                pe.matmul(bank[:, 0:256], f_hth[s % 3][:, r],
                          w2[:, bass.ds(e * 4 + f, 1), :].rearrange("p a n -> p (a n)"), start=(f == 0), stop=False)
                pe.matmul(o, f_htl[s % 3][:, r],
                          w2[:, bass.ds(e * 4 + f, 1), 0:128].rearrange("p a n -> p (a n)"), start=False, stop=False)
            i = pe.matmul(o, f_sel[:, s:s + 1].broadcast_to((128, 128)), b2s[:, :], start=False, stop=True)
            k = k_ym[s] = c_pe.up(i)
            wait(dve, k)
            k_y[s] = c_dve.up(dve.tensor_reduce(f_ys[:, s, :], bank[:, 0:256].rearrange("p (h d) -> p d h", h=2),
                                                AX, ALU.add))

        def back(s):
            wait(pool, k_y[s])
            return c_ys.up(pool.indirect_dma_start(
                ys_dram, bass.IndirectOffsetOnAxis(ap=f_xs[:, s, 128:129].bitcast(U32), axis=0), f_ys[:, s, :], None,
                bounds_check=NT * 128 - 1, oob_is_err=False))

        XT(0)
        XT(1)
        for s in range(NS + 3):
            if s < NS:
                H(s)
            if s % 4 == 3 and s // 4 + 2 < 6:
                XT(s // 4 + 2)
            if 1 <= s <= NS:
                HT(s - 1)
            if s >= 3:
                Y(s - 3)
                d = back(s - 3)
        ysv = ys_dram.rearrange("(s p) d -> p s d", p=128)
        d_yt = [load(xn[:, 4 * g:4 * g + 4, 0:128], ysv[:, 4 * g:4 * g + 4, :], eng=(sp, act)[g % 2], after=[d])
                for g in range(4)]
        barrier()
        marks = []
        for j in range(NT):
            wait(dve, d_yt[j // 4])
            k = c_dve.up(dve.scalar_tensor_tensor(x[:, j, :], xn[:, j, 0:128], gate[:, j:j + 1], x[:, j, :],
                                                  ALU.mult, ALU.add))
            marks.append(k)
            finish(j, k)
        return marks

    def all_done():
        return [(c, c.n) for c in (c_pe, c_dve, c_act, c_pool) if c.n]

    def barrier():
        m = all_done()
        for eng in (pe, dve, act, pool, sp):
            wait(eng, *m)

    barrier()
    start_rows()

    def extra_a(s):
        if s % 3 == 0 and s // 3 < 16:
            stage_load(s // 3)
        if s % 3 == 1 and s // 3 < 16:
            stage_split(s // 3)
        if s % 3 == 2 and s // 3 < 16:
            stage_low(s // 3)
        if s == 50:
            stage_bias(t["b1"], b1s, 512)
        if s == 56:
            stage_bias(t["b2"], b2s, 128)

    TA = a_TA

    def table_a(h, it):
        if it == 1:
            return TA[:, 256 * h:256 * h + 256]
        o = TA[:, 256 * h + 128:256 * h + 256]
        return bass.AP(o.tensor, o.offset, [list(o.ap[0]), [4096 - 256 * h - 128, 2], [1, 128]])

    attention(False, lambda b: d_x, k_weights, table_a, k_T, extra_a)
    barrier()

    d_bq = load(bq[:, :], t["w_q"])
    d_bu = load(bu[:, :], t["w_kv_up"])
    d_bd = load(bkd[:, :], t["w_kv_down"])
    d_bo = load(bo[:, :, :], t["w_out_b"].rearrange("(c p) n -> p c n", p=128))
    k_wb = []

    def weights_b():
        n = 0
        for src, dst, d in ((bq, bqT, d_bq), (bu, bkT, d_bu)):
            for g in range(2):
                bank = ps[2 + n]
                n += 1
                wait(pe, d)
                for j in range(4):
                    i = tr(bank[:, 128 * j:128 * j + 128], src[:, 512 * g + 128 * j:512 * g + 128 * j + 128])
                k = c_pe.up(i)
                wait(act, k)
                k = c_act.up(act.copy(dst[:, 4 * g:4 * g + 4, :], bank[:, :].rearrange("p (a b) -> p a b", a=4)))
        wait(pe, k)
        k_wb.extend(products(bqT, bkT, ps[2:6]))
        k_wb.extend(split(wvh[:, :], wvl[:, :], bu[:, 1024:2048], [d_bu]))
        k_wb.extend(split(wo[:, :, 0:128], wo[:, :, 128:256], bo[:, :, :], [d_bo]))
        k_wb.extend(split(kdh[:, :], kdl[:, :], bkd[:, :], [d_bd]))
        wait(pe, *k_wb)

    k_x2 = experts(lambda j, k: None, weights_b)
    start_rows()

    CM = b_cm[:, :]
    k = c_pool.up(pool.memset(CM, 0.0))
    wait(pool, k)
    k_cm = c_pool.up(pool.affine_select(out=CM, in_=CM, compare_op=ALU.is_ge, fill=MASKED, base=128,
                                        pattern=[[-1, 256]], channel_multiplier=1))
    attention(True, lambda b: k_x2[2 * b + 1], k_wb,
                           lambda h, it: CM if it == 1 else CM[:, 128:256], k_cm, lambda s: None)
    barrier()
    c_o = dma_sem()
    last = []

    def finish(j, k):
        if j % 4 == 3:
            last.append(load(ov[:, j - 3:j + 1, :], x[:, j - 3:j + 1, :], after=[k], c=c_o))

    experts(finish, lambda: None)
    wait(sp, last[-1])
    ctx.close()


_INS = ["L0_attn_a_x", "L0_attn_a_w_qkv", "L0_attn_a_w_out", "L0_attn_b_w_kv_down", "L0_attn_b_w_kv_up",
        "L0_attn_b_w_q", "L0_attn_b_w_out", "L0_ffn_Wr", "L0_ffn_br", "L0_ffn_ln_g", "L0_ffn_ln_b",
        "L0_ffn_W1", "L0_ffn_b1", "L0_ffn_W2", "L0_ffn_b2"]
_SHORT = {"L0_attn_a_x": "x", "L0_attn_a_w_qkv": "w_qkv", "L0_attn_a_w_out": "w_out_a",
          "L0_attn_b_w_kv_down": "w_kv_down", "L0_attn_b_w_kv_up": "w_kv_up", "L0_attn_b_w_q": "w_q",
          "L0_attn_b_w_out": "w_out_b", "L0_ffn_Wr": "Wr", "L0_ffn_br": "br", "L0_ffn_ln_g": "ln_g",
          "L0_ffn_ln_b": "ln_b", "L0_ffn_W1": "W1", "L0_ffn_b1": "b1", "L0_ffn_W2": "W2", "L0_ffn_b2": "b2"}


def kernel(**inputs):
    import concourse.bacc as bacc
    from concourse.bass_utils import run_bass_kernel_spmd

    nc = bacc.Bacc("TRN2", target_bir_lowering=False, num_devices=1)
    arrays, t = {}, {}

    def give(name, a):
        arrays[f"in_{name}"] = a
        t[name] = nc.dram_tensor(f"in_{name}", a.shape, mybir.dt.from_np(a.dtype), kind="ExternalInput").ap()

    for name in _INS:
        a = np.ascontiguousarray(inputs[name])
        give(_SHORT[name], a)
    rel = np.ascontiguousarray(inputs["L0_attn_a_rel_bias"])
    index = np.minimum(127 + np.arange(256)[None, :] - np.arange(128)[:, None], 254)
    give("bias", np.ascontiguousarray(rel[index].transpose(0, 2, 1)))
    t["out"] = nc.dram_tensor("out_0", (8, 256, 128), F32, kind="ExternalOutput").ap()
    build(nc, t)
    r = run_bass_kernel_spmd(nc, [arrays], core_ids=[0])
    return r.results[0]["out_0"]
```

```python
from contextlib import ExitStack

import numpy as np

import concourse.bass as bass
from concourse import mybir

F32 = mybir.dt.float32
F32R = mybir.dt.float32r
I32 = mybir.dt.int32
U32 = mybir.dt.uint32
ALU = mybir.AluOpType
ACT = mybir.ActivationFunctionType
AX = mybir.AxisListType.X

NT = 16
NB = 8
NC = 8
NE = 8
NS = 23
REG = 2048 + 128
XROWS = NE * REG + 7 * 128
NOWHERE = 1 << 20
EPS = 1e-5
BIG = 3.0e38
MASKED = 1.0e30


class Counter:

    def __init__(self, handle, step=1):
        self.handle, self.step, self.n = handle, step, 0

    def up(self, ins):
        ins.then_inc(self.handle, self.step)
        self.n += self.step
        return self, self.n


class Waits:

    def __init__(self):
        self.seen = {}

    def __call__(self, eng, *marks):
        for m in marks:
            if m is None:
                continue
            c, v = m
            key = (eng.engine, c)
            if self.seen.get(key, 0) < v:
                eng.wait_ge(c.handle, v)
                self.seen[key] = v


def build(nc, t):
    pe, dve, act, pool, sp = nc.tensor, nc.vector, nc.scalar, nc.gpsimd, nc.sync
    ctx = ExitStack()
    names = [0]

    def sem(name, step=1):
        return Counter(ctx.enter_context(nc.semaphore(name)), step)

    wait = Waits()
    c_pe, c_dve, c_act, c_pool = sem("c_pe"), sem("c_dve"), sem("c_act"), sem("c_pool")

    def sb(name, shape, dt=F32, scope=None):
        return (scope or ctx).enter_context(nc.sbuf_tensor(name, shape, dt))

    def dma_sem():
        names[0] += 1
        return sem(f"d{names[0]}", 16)

    class Spare:

        def __init__(self):
            self.free, self.n = {3: None, 7: None}, 3

        def take(self):
            self.n = 10 - self.n
            wait(pe, self.free[self.n])
            return ps[self.n], self.n

    spare = Spare()

    def load(dst, src, eng=None, after=(), c=None):
        eng = eng or sp
        wait(eng, *after)
        c = c or dma_sem()
        return c.up(eng.dma_start(dst, src))

    ps = [ctx.enter_context(nc.psum_tensor(f"ps{i}", [128, 512], F32)) for i in range(8)]
    PT_ = ps[0]
    PS = ps[1:3]
    PP = ps[4:6]
    PO = ps[6]

    xs_dram = nc.dram_tensor("xs_scratch", (XROWS, 129), F32).ap()
    ys_dram = nc.dram_tensor("ys_scratch", (NT * 128, 128), F32).ap()
    c_sc, c_ys, c_pad, c_pad2 = dma_sem(), dma_sem(), dma_sem(), dma_sem()
    d_row = [None]

    x = sb("x", [128, NT, 128])
    w1h, w1l = sb("w1h", [128, NE * 512], F32R), sb("w1l", [128, NE * 512], F32R)
    w2 = sb("w2", [128, NE * 4, 256], F32R)
    b1s = sb("b1s", [128, 512], F32R)
    b2s = sb("b2s", [128, 128], F32R)
    pid = sb("pid", [128, 1])
    pidi = sb("pidi", [128, 1], I32)
    xn = sb("xn", [128, NT, 129])
    gate = sb("gate", [128, NT])
    posi = sb("posi", [128, NT], I32)
    posf = sb("posf", [128, 4])
    run, runi = sb("run", [128, NE]), sb("runi", [128, NE], I32)
    bas, hot = sb("bas", [128, 4, NE]), sb("hot", [128, 4, NE])
    gmx, cnt = sb("gmx", [128, 4]), sb("cnt", [128, 64])
    padt = sb("padt", [128, 129])
    mh, ml = sb("mh", [128, 16 * 128], F32R), sb("ml", [128, 16 * 128], F32R)
    wvh, wvl = sb("wvh", [128, 1024], F32R), sb("wvl", [128, 1024], F32R)
    wo = sb("wo", [128, 8, 256], F32R)
    ident = sb("ident", [128, 128])
    tri = sb("tri", [128, 128])
    ones = sb("ones", [128, 128])
    lng, lnb = sb("lng", [128, 128]), sb("lnb", [128, 128])
    brb = sb("brb", [128, NE])
    wr = sb("wr", [128, NE])
    half = sb("half", [128, 16])
    stats = sb("stats", [128, 2, 6])
    mv = sb("mv", [128, 2, 2])
    rstd = sb("rstd", [128, 2])
    kdh, kdl = sb("kdh", [128, 128], F32R), sb("kdl", [128, 128], F32R)
    lg = sb("lg", [128, NT, NE])

    iota_i = sb("iota_i", [128, 32], I32)
    iota_e = sb("iota_e", [128, NE])
    iota_k = sb("iota_k", [128, 16])
    iota_s = sb("iota_s", [128, NS])
    cT = sb("cT", [128, 16])

    base = ExitStack()
    a_ring = [sb(f"ring{i}", [128, 2, 2, 256], scope=base) for i in range(3)]
    a_pt = [sb(f"pt{i}", [128, 2, 512], scope=base) for i in range(2)]
    a_th = [sb(f"th{i}", [128, 512], F32R, scope=base) for i in range(2)]
    a_tl = [sb(f"tl{i}", [128, 512], F32R, scope=base) for i in range(2)]
    bt = ExitStack()
    bqT = sb("bqT", [128, 8, 128], scope=bt)
    bkT = sb("bkT", [128, 8, 128], scope=bt)
    bt.close()
    a_v = [sb(f"v{i}", [128, 2, 1024], scope=base) for i in range(2)]
    pre_o = ExitStack()
    won = sb("won", [128, 1024], scope=pre_o)
    pre_o.close()
    a_oh = sb("oh", [128, 8, 256], F32R, scope=base)
    a_ol = sb("ol", [128, 8, 256], F32R, scope=base)
    a_xh = sb("xh", [128, 2, 128], scope=base)
    a_ph = sb("ph", [128, 2, 128], scope=base)
    a_oT = sb("oT", [128, 256], scope=base)
    a_pT = sb("pT", [128, 256], scope=base)
    a_xth = [sb(f"xth{i}", [128, 256], F32R, scope=base) for i in range(2)]
    a_xtl = [sb(f"xtl{i}", [128, 256], F32R, scope=base) for i in range(2)]
    a_mn = [sb(f"mn{i}", [128, 4], scope=base) for i in range(3)]
    a_sm = [sb(f"sm{i}", [128, 4], scope=base) for i in range(3)]
    a_rs = [sb(f"rs{i}", [128, 4], scope=base) for i in range(3)]
    s2 = sb("s2", [128, 2, 6], scope=base)
    m2 = sb("m2", [128, 2, 2], scope=base)
    r2 = sb("r2", [128, 2], scope=base)
    b_only = ExitStack()
    a_lth = [sb(f"lth{i}", [128, 256], F32R, scope=b_only) for i in range(2)]
    a_ltl = [sb(f"ltl{i}", [128, 256], F32R, scope=b_only) for i in range(2)]
    b_cm = sb("cm", [128, 256], scope=b_only)
    b_only.close()
    bw = ExitStack()
    bq = sb("bq", [128, 1024], scope=bw)
    bu = sb("bu", [128, 2048], scope=bw)
    bkd = sb("bkd", [128, 128], scope=bw)
    bo = sb("bo", [128, 8, 128], scope=bw)
    bw.close()
    a_TA = sb("T", [128, 16 * 256 + 128], scope=base)
    a_T = a_TA[:, 0:4096].rearrange("p (h n) -> p h n", h=16)
    stage = [sb("stage", [128, 512], scope=base)]
    base.close()

    pre = ExitStack()
    wqn = sb("wqn", [128, 8, 128], scope=pre)
    wkn = sb("wkn", [128, 8, 128], scope=pre)
    wvn = sb("wvn", [128, 8, 128], scope=pre)
    pre.close()

    fs = ExitStack()
    f_xs = sb("f_xs", [128, NS, 129], scope=fs)
    f_ys = sb("f_ys", [128, NS, 128], scope=fs)
    f_xth = [sb(f"f_xth{i}", [128, 512], F32R, scope=fs) for i in range(2)]
    f_xtl = [sb(f"f_xtl{i}", [128, 512], F32R, scope=fs) for i in range(2)]
    f_h = [sb(f"f_h{i}", [128, 512], scope=fs) for i in range(2)]
    f_b1 = sb("f_b1", [128, 4, NS], scope=fs)
    f_h2 = [sb(f"f_h2{i}", [128, 512], scope=fs) for i in range(2)]
    f_hth = [sb(f"f_hth{i}", [128, 512], F32R, scope=fs) for i in range(3)]
    f_htl = [sb(f"f_htl{i}", [128, 512], F32R, scope=fs) for i in range(3)]
    f_e = [sb(f"f_e{i}", [128, NE], scope=fs) for i in range(6)]
    f_g, f_g2 = sb("f_g", [128, NS, NE], scope=fs), sb("f_g2", [128, NS, NE], scope=fs)
    f_k16 = sb("f_k16", [128, NE, 16], scope=fs)
    f_row, f_ri = sb("f_row", [128, NS], scope=fs), sb("f_ri", [128, NS], I32, scope=fs)
    f_ei = sb("f_ei", [128, NS], I32, scope=fs)
    f_sub = sb("f_sub", [128, NT, NE], scope=fs)
    f_ef = sb("f_ef", [128, NS + 1], scope=fs)
    f_sel = sb("f_sel", [128, NS + 1], F32R, scope=fs)
    fs.close()


    xv = t["x"].rearrange("b (s p) d -> p (b s) d", p=128)
    ov = t["out"].rearrange("b (s p) d -> p (b s) d", p=128)
    wq3 = t["w_qkv"].rearrange("(d c h) x -> c d h x", c=3, h=16)
    c_w, c_wv = dma_sem(), dma_sem()
    for j, w in enumerate((wqn, wkn)):
        for hh in range(2):
            d_w = load(w[64 * hh:64 * hh + 64, :, :], wq3[j, :, hh::2, :], c=c_w, eng=act if hh else sp)
    d_x0 = load(x[:, 0:2, :], xv[:, 0:2, :])
    for hh in range(2):
        d_wv = load(wvn[64 * hh:64 * hh + 64, :, :], wq3[2, :, hh::2, :], c=c_wv, eng=act if hh else sp)
    d_T = [load(a_T[:, 0:4, :], t["bias"][:, 0:4, :]),
           load(a_T[:, 4:16, :], t["bias"][:, 4:16, :], eng=act)]
    d_won = load(won[:, :], t["w_out_a"])
    d_x = load(x[:, 2:16, :], xv[:, 2:16, :])
    d_wr = load(wr[:, :], t["Wr"])
    c_b = dma_sem()
    load(lng[:, :], t["ln_g"].rearrange("(a d) -> a d", a=1).broadcast_to((128, 128)), c=c_b)
    load(lnb[:, :], t["ln_b"].rearrange("(a d) -> a d", a=1).broadcast_to((128, 128)), c=c_b)
    d_b = load(brb[:, :], t["br"].rearrange("(a d) -> a d", a=1).broadcast_to((128, NE)), c=c_b)

    def setup(ins):
        k = c_pool.up(ins)
        wait(pool, k)
        return k

    setup(pool.memset(ident[:, :], 0.0))
    k_id = setup(pool.affine_select(out=ident[:, :], in_=ident[:, :], compare_op=ALU.not_equal, fill=1.0,
                                    base=0, pattern=[[-1, 128]], channel_multiplier=1))
    k_h = setup(pool.memset(half[:, :], -0.5))
    setup(pool.memset(ones[:, :], 1.0))
    k_tri = setup(pool.affine_select(out=tri[:, :], in_=ones[:, :], compare_op=ALU.is_gt, fill=0.0,
                                     base=0, pattern=[[1, 128]], channel_multiplier=-1))
    k_T0 = setup(pool.memset(a_TA[:, 4096:4224], 0.0))
    setup(pool.memset(b1s[:, :].bitcast(F32), 0.0))
    k_b0 = setup(pool.memset(b2s[:, :].bitcast(F32), 0.0))
    setup(pool.memset(pid[:, :], -1.0))
    for row in (0, 32):
        setup(pool.iota(pidi[row:row + NE, :], pattern=[[0, 1]], base=0, channel_multiplier=1))
        k_pid = setup(pool.tensor_copy(pid[row:row + NE, :], pidi[row:row + NE, :]))
    setup(pool.iota(iota_i[:, :], pattern=[[1, 32]], base=0, channel_multiplier=0))
    setup(pool.tensor_copy(iota_s[:, :], iota_i[:, 0:NS]))
    setup(pool.tensor_scalar(iota_k[:, :], iota_i[:, 0:16], 128.0, 0.0, ALU.mult, ALU.add))
    k_iota = setup(pool.tensor_scalar(iota_e[:, :], iota_i[:, 0:NE], -1.0, float(NE), ALU.mult, ALU.add))
    setup(pool.memset(padt[:, 0:128], 0.0))
    k_padt = setup(pool.memset(padt[:, 128:129].bitcast(I32), NOWHERE))
    k_tok = setup(pool.iota(xn[:, :, 128:129].bitcast(I32).rearrange("p t a -> p (t a)"), pattern=[[128, NT]], base=0,
                            channel_multiplier=1))
    d_empty = load(xs_dram[NE * REG:XROWS, :].rearrange("(k p) d -> p k d", p=128),
                   padt[:, :].rearrange("p (k d) -> p k d", k=1).broadcast_to((128, 7, 129)), after=[k_padt])

    def split(high, low, src, after, scale=None, he=act, le=dve):
        wait(he, *after)
        cnt = {id(act): c_act, id(dve): c_dve, id(pool): c_pool}
        if he is act:
            i = act.activation(high, src, ACT.Copy, scale=1.0 if scale is None else scale)
        else:
            i = he.tensor_copy(high, src)
        a = cnt[id(he)].up(i)
        wait(le, a, *after)
        if scale is None:
            i = le.tensor_tensor(low, src, high.bitcast(F32), ALU.subtract)
        else:
            i = le.scalar_tensor_tensor(low, src, scale, high.bitcast(F32), ALU.mult, ALU.subtract)
        return a, cnt[id(le)].up(i)

    def three(out, ah, al, bh, bl, first=True, last=True):
        pe.matmul(out, ah, bh, start=first, stop=False)
        pe.matmul(out, al, bh, start=False, stop=False)
        return pe.matmul(out, ah, bl, start=False, stop=last)

    def tr(out, src):
        return pe.transpose(out, src, ident[:, :])

    def product(q, k, n, bank):
        g, hh = divmod(n, 2)
        rows = slice(64 * hh, 64 * hh + 64)
        for j in range(4):
            i = pe.matmul(bank[:, 128 * j:128 * j + 128], q[rows, 4 * g + j, :], k[rows, 4 * g + j, :],
                          start=True, stop=True)
        m = c_pe.up(i)
        v = [w[:, :].rearrange("p (c h n) -> p h c n", h=2, n=128)[:, hh, 4 * g:4 * g + 4, :] for w in (mh, ml)]
        return split(*v, bank[:, :].rearrange("p (c n) -> p c n", c=4), [m], scale=-0.125)

    k_ma = []

    def weights_a1():
        wait(pe, d_w)
        for n in range(2):
            k_ma.append(product(wqn, wkn, n, ps[n]))

    def weights_a2():
        for n in range(2, 4):
            k_ma.append(product(wqn, wkn, n, ps[n]))
        wait(pe, d_wv, k_id)
        for g in range(2):
            bank = ps[4 + g]
            for j in range(4):
                i = tr(bank[:, 128 * j:128 * j + 128], wvn[:, 4 * g + j, :])
            k = c_pe.up(i)
            r = slice(512 * g, 512 * g + 512)
            k_va.extend(split(wvh[:, r], wvl[:, r], bank[:, :], [k]))

    def weights_a3(*gs):
        wait(pe, d_won)
        for g in gs:
            bank, n = spare.take()
            for j in range(4):
                i = tr(bank[:, 128 * j:128 * j + 128], won[:, 512 * g + 128 * j:512 * g + 128 * j + 128])
            k = c_pe.up(i)
            w = wo[:, 4 * g:4 * g + 4, :]
            k_oa.extend(split(w[:, :, 0:128], w[:, :, 128:256], bank[:, :].rearrange("p (c n) -> p c n", c=4), [k]))
            spare.free[n] = k_oa[-1]

    k_va, k_oa = [], []

    def bias_ready(u):
        if u < 8:
            wait(dve, d_T[u >= 2], k_T0)
            v, e = a_T[:, 2 * u:2 * u + 2, :], cT[:, 2 * u:2 * u + 2]
            k = c_dve.up(dve.tensor_copy(e, v[:, :, 255:256].rearrange("p a b -> p (a b)")))
            wait(dve, k)
            k_T[0] = c_dve.up(dve.tensor_tensor(v, e.rearrange("p (a b) -> p a b", b=1).broadcast_to((128, 2, 256)),
                                                v, ALU.subtract))
        return k_T[0]

    k_T = [None]

    stage_free = [None]
    chunks = []
    for e in range(NE):
        r = slice(512 * e, 512 * e + 512)
        chunks.append((w1h[:, r], w1l[:, r], t["W1"][e]))
        w = w2[:, 4 * e:4 * e + 4, :]
        chunks.append((w[:, :, 0:128], w[:, :, 128:256], t["W2"][e].rearrange("(c p) d -> p c d", p=128)))
    c_st = [dma_sem()]
    k_high = [None]
    k_ff, k_fb = [None], [None]

    def stage_load(n):
        s = stage[0]
        h, l, src = chunks[n]
        dst = s[:, :] if len(src.shape) == 2 else s[:, :].rearrange("p (c d) -> p c d", c=4)
        d_stage[n] = load(dst, src, after=[stage_free[0]], c=c_st[0])

    def stage_split(n):
        s = stage[0]
        h, l, src = chunks[n]
        v = s[:, :] if len(src.shape) == 2 else s[:, :].rearrange("p (c d) -> p c d", c=4)
        wait(act, d_stage[n])
        k_high[0] = c_act.up(act.copy(h, v))

    def stage_low(n):
        s = stage[0]
        h, l, src = chunks[n]
        v = s[:, :] if len(src.shape) == 2 else s[:, :].rearrange("p (c d) -> p c d", c=4)
        wait(dve, k_high[0], d_stage[n])
        stage_free[0] = c_dve.up(dve.tensor_tensor(l, v, h.bitcast(F32), ALU.subtract))
        k_ff[0] = stage_free[0]

    d_stage = {}

    def stage_bias(src, dst, w):
        s, c = stage[0], c_st[0]
        for row in (0, 32):
            d = load(s[row:row + NE, 0:w], src, after=[stage_free[0]], c=c)
        wait(dve, d, k_b0)
        for row in (0, 32):
            k = c_dve.up(dve.tensor_copy(dst[row:row + NE, :], s[row:row + NE, 0:w]))
        wait(dve, k)
        stage_free[0] = k_fb[0] = c_dve.up(dve.tensor_tensor(
            dst[32:32 + NE, :], s[32:32 + NE, 0:w], dst[32:32 + NE, :].bitcast(F32), ALU.subtract))

    def norm_a(src, st, m, r, after):
        wait(dve, *after)
        for j in range(2):
            k = c_dve.up(dve.bn_stats(st[:, j, :], src[:, j, :]))
        wait(dve, k)
        for j in range(2):
            k = c_dve.up(dve.bn_aggr(m[:, j, :], st[:, j, :]))
        wait(dve, k)
        k = c_dve.up(dve.tensor_scalar(r[:, :], m[:, :, 1], EPS, None, ALU.add))
        wait(pool, k, k_h)
        return c_pool.up(pool.tensor_tensor(r[:, :], r[:, :], half[:, 0:2], ALU.pow))

    def norm_b(dst, src, m, r, k, *after):
        wait(dve, k, *after)
        for j in range(2):
            k = c_dve.up(dve.tensor_scalar(dst[:, j, :], src[:, j, :], m[:, j, 0:1], r[:, j:j + 1],
                                           ALU.subtract, ALU.mult))
        return k

    def gain(dst, k):
        wait(pool, k, d_b)
        bc = lambda a: a[:, :].rearrange("p (a d) -> p a d", a=1).broadcast_to((128, 2, 128))
        k = c_pool.up(pool.tensor_tensor(dst, dst, bc(lng), ALU.mult))
        wait(pool, k)
        return c_pool.up(pool.tensor_tensor(dst, dst, bc(lnb), ALU.add))

    ACT_COPIES = (0, 2, 6)

    def attention(stage_b, x_ready, T_w, V_w, O_w, table, table_ready, extra, first, second):
        causal = stage_b
        xT, lT, V = {}, {}, {}
        k_T_, k_tH, k_tL, k_S, k_mn, k_exp, k_nrm, k_TR, k_PT, k_PV, k_O, k_OH = ({} for _ in range(12))
        k_out, k_xh_free, k_post = {}, [None], {}
        k_x = {}
        last_T = {}

        k_r1 = {}

        def pre_a(b):
            k_r1[b] = norm_a(x[:, 2 * b:2 * b + 2, :], stats, mv, rstd, [x_ready(b), k_x.get(b - 1)])

        def pre_a2(b):
            k_x[b] = norm_b(a_xh, x[:, 2 * b:2 * b + 2, :], mv, rstd, k_r1[b], k_xh_free[0])

        def pre_b(b):
            PX, n = spare.take()
            wait(pe, k_x[b], k_id)
            for j in range(2):
                i = tr(PX[:, 128 * j:128 * j + 128], a_xh[:, j, :])
            k = c_pe.up(i)
            k_xh_free[0] = k
            gone = ([k_lat.get(b - 2), k_T_.get(8 * (b - 2) + 7)] if stage_b
                    else [k_S.get(8 * (b - 2) + 7), k_V.get((b - 2, 3))])
            xT[b] = split(a_xth[b % 2][:, :], a_xtl[b % 2][:, :], PX[:, 0:256], [k, *gone])
            spare.free[n] = xT[b][1]

        k_lat = {}
        k_V = {}

        def pre_c(b):
            PX, n = spare.take()
            wait(pe, *xT[b], *V_w)
            k = k_lat[b] = c_pe.up(three(PX[:, 0:256], kdh[:, :], kdl[:, :], a_xth[b % 2][:, :], a_xtl[b % 2][:, :]))
            lT[b] = split(a_lth[b % 2][:, :], a_ltl[b % 2][:, :], PX[:, 0:256],
                          [k, k_S.get(8 * (b - 2) + 7), k_V.get((b - 2, 3))])
            spare.free[n] = lT[b][1]

        def key(b):
            return (a_lth, a_ltl, lT) if stage_b else (a_xth, a_xtl, xT)

        def values(b, n):
            H, L, marks = key(b)
            j, half_ = n // 2, n % 2
            PX, m = spare.take()
            wait(pe, *marks[b], *V_w)
            r = slice(512 * half_, 512 * half_ + 512)
            c = slice(128 * j, 128 * j + 128)
            k = k_V[(b, n)] = c_pe.up(three(PX[:, :], H[b % 2][:, c], L[b % 2][:, c], wvh[:, r], wvl[:, r]))
            wait(act, k, k_PV.get(8 * (b - 2) + 7))
            spare.free[m] = V[(b, n)] = c_act.up(act.copy(a_v[b % 2][:, j, r], PX[:, :]))

        def T(u):
            b, c = divmod(u, 8)
            wait(pe, *xT[b], k_tL.get(u - 1))
            for hh in range(2):
                wait(pe, *T_w(2 * (c // 4) + hh))
                h = 2 * c + hh
                r = slice(128 * h, 128 * h + 128)
                i = three(PT_[:, 256 * hh:256 * hh + 256], mh[:, r], ml[:, r], a_xth[b % 2][:, :], a_xtl[b % 2][:, :])
            k = k_T_[u] = c_pe.up(i)
            k_tH[u], k_tL[u] = split(a_th[u % 2][:, :], a_tl[u % 2][:, :], PT_[:, :], [k, k_S.get(u - 2)])

        def S(u):
            b, c = divmod(u, 8)
            H, L, marks = key(b)
            wait(pe, k_tH[u], k_tL[u], *marks[b])
            ring, mn, sm, rs = a_ring[u % 3], a_mn[u % 3], a_sm[u % 3], a_rs[u % 3]
            k_table = table_ready(u)
            for hh in range(2):
                n = 2 * u + hh
                bank = PS[n % 2]
                wait(pe, k_mn.get(n - 2))
                for it in range(2):
                    w = 128 if causal and it == 0 else 256
                    q = slice(256 * hh + 128 * it, 256 * hh + 128 * it + 128)
                    i = three(bank[:, 256 * it:256 * it + w], a_th[u % 2][:, q], a_tl[u % 2][:, q],
                              H[b % 2][:, 0:w], L[b % 2][:, 0:w])
                k = c_pe.up(i)
                wait(dve, k, k_TR.get(2 * (u - 3) + hh), k_table)
                for it in range(2):
                    w = 128 if causal and it == 0 else 256
                    k2 = c_dve.up(dve.tensor_tensor_reduce(
                        ring[:, hh, it, 0:w], bank[:, 256 * it:256 * it + w], table(2 * c + hh, it), 1.0, BIG,
                        ALU.add, ALU.min, mn[:, 2 * hh + it:2 * hh + it + 1]))
                k_mn[n] = k2
            k_S[u] = k

        def expo(u):
            ring, mn, sm = a_ring[u % 3], a_mn[u % 3], a_sm[u % 3]
            for hh in range(2):
                wait(act, k_mn[2 * u + hh], *k_nrm.get(u - 3, ()))
                for it in range(2):
                    w = 128 if causal and it == 0 else 256
                    q = slice(2 * hh + it, 2 * hh + it + 1)
                    k3 = c_act.up(act.activation(ring[:, hh, it, 0:w], ring[:, hh, it, 0:w], ACT.Exp,
                                                 bias=mn[:, q], scale=-1.0, accum_out=sm[:, q]))
            k_exp[u] = k3

        def weigh(u):
            ring, sm, rs = a_ring[u % 3], a_sm[u % 3], a_rs[u % 3]
            k3 = k_exp[u]
            wait(dve, k3)
            k4 = c_dve.up(dve.reciprocal(rs[:, :], sm[:, :]))
            wait(pool, k4, k3)
            wait(dve, k4)
            k5 = {}
            for hh in range(2):
                for it in range(2):
                    w = 128 if causal and it == 0 else 256
                    q = slice(2 * hh + it, 2 * hh + it + 1)
                    eng, cnt = (dve, c_dve) if hh and u > 8 * NB - 4 else (pool, c_pool)
                    k5[cnt] = cnt.up(eng.tensor_scalar(ring[:, hh, it, 0:w], ring[:, hh, it, 0:w], rs[:, q], 1.0,
                                                       ALU.mult, ALU.mult))
            k_nrm[u] = list(k5.values())

        def TR(u):
            ring = a_ring[u % 3]
            wait(pe, *k_nrm[u])
            for hh in range(2):
                n = 2 * u + hh
                bank = PP[hh]
                wait(pe, k_PT.get(n - 2))
                for jt in range(2):
                    for it in range(2):
                        if causal and jt > it:
                            continue
                        i = tr(bank[:, 256 * jt + 128 * it:256 * jt + 128 * it + 128],
                               ring[:, hh, it, 128 * jt:128 * jt + 128])
                k = k_TR[n] = c_pe.up(i)
                on_dve = hh and (u + 4) % 8 not in ACT_COPIES
                eng, cnt = (dve, c_dve) if on_dve else (act, c_act)
                wait(eng, k, k_PV.get(u - 2))
                cp = dve.tensor_copy if on_dve else act.copy
                if causal:
                    cp(a_pt[u % 2][:, hh, 0:256], bank[:, 0:256])
                    k_PT[n] = cnt.up(cp(a_pt[u % 2][:, hh, 384:512], bank[:, 384:512]))
                else:
                    k_PT[n] = cnt.up(cp(a_pt[u % 2][:, hh, :], bank[:, :]))

        def PV(u):
            b, c = divmod(u, 8)
            wait(pe, k_PT[2 * u], k_PT[2 * u + 1], V[(b, 3)], k_O.get(u - 1))
            for jt in range(2):
                lo = 128 if causal and jt == 1 else 0
                for hh in range(2):
                    i = pe.matmul(PO[64 * hh:64 * hh + 64, lo:256],
                                  a_v[b % 2][:, jt, 128 * c + 64 * hh:128 * c + 64 * hh + 64],
                                  a_pt[u % 2][:, hh, 256 * jt + lo:256 * jt + 256], start=(jt == 0), stop=(jt == 1))
            k_PV[u] = c_pe.up(i)

        def keep(u):
            b, c = divmod(u, 8)
            k_OH[u], k_O[u] = split(a_oh[:, c, :], a_ol[:, c, :], PO[:, 0:256], [k_PV[u], k_out.get(b - 1)])

        def out_last(*cs):
            b = NB - 1
            wait(pe, k_mn[16 * NB - 1], *O_w)
            for c in cs:
                wait(pe, k_O[8 * b + c], k_OH[8 * b + c])
                for j in range(2):
                    r = slice(128 * j, 128 * j + 128)
                    pe.matmul(PS[j][:, 0:256], a_oh[:, c, r], wo[:, c, :], start=(c == 0), stop=False)
                    i = pe.matmul(PS[j][:, 0:128], a_ol[:, c, r], wo[:, c, 0:128], start=False, stop=(c == 7))
            if c == 7:
                k = k_out[b] = c_pe.up(i)
                xx = x[:, 2 * b:2 * b + 2, :]
                wait(dve, k, k_x[b])
                for h in range(2):
                    for j in range(2):
                        k = c_dve.up(dve.tensor_tensor(xx[:, j, :], PS[j][:, 128 * h:128 * h + 128], xx[:, j, :],
                                                       ALU.add))
                    wait(dve, k)
                k_post[b] = norm_a(xx, s2, m2, r2, [k])

        def out(b):
            PX, n = spare.take()
            wait(pe, k_O[8 * b + 7], k_OH[8 * b + 7], *O_w)
            for c in range(8):
                i = three(PX[:, 0:256], wo[:, c, 0:128], wo[:, c, 128:256], a_oh[:, c, :], a_ol[:, c, :],
                          first=(c == 0), last=(c == 7))
            k = k_out[b] = c_pe.up(i)
            wait(act, k, k_oT[1])
            k_oT[0] = spare.free[n] = c_act.up(act.copy(a_oT[:, :], PX[:, 0:256]))

        k_oT = [None, None]

        def out_2(b):
            PX, n = spare.take()
            wait(pe, k_oT[0])
            for j in range(2):
                i = tr(PX[:, 128 * j:128 * j + 128], a_oT[:, 128 * j:128 * j + 128])
            k = k_oT[1] = c_pe.up(i)
            xx = x[:, 2 * b:2 * b + 2, :]
            wait(dve, k, k_x[b])
            k = spare.free[n] = c_dve.up(dve.tensor_tensor(xx, PX[:, 0:256].rearrange("p (a d) -> p a d", a=2), xx,
                                                           ALU.add))
            k_post[b] = norm_a(xx, s2, m2, r2, [k])

        def post_a(b):
            k = k_post[b] = norm_b(a_ph, x[:, 2 * b:2 * b + 2, :], m2, r2, k_post[b], k_phpe[0], k_phdve[0])
            k_lg2[b] = norm_a(a_ph, s2, m2, r2, [k])

        def post_a2(b):
            xx = xn[:, 2 * b:2 * b + 2, 0:128]
            k = k_phdve[0] = norm_b(xx, a_ph, m2, r2, k_lg2[b])
            k_xn[b] = gain(xx, k)

        k_lg2, k_xn, k_hot, k_pre = {}, {}, {}, {}
        k_phdve, k_pT_free, k_pT, k_phpe = [None], [None], [None], [None]

        def post_b(b):
            PX, n = spare.take()
            wait(pe, k_post[b])
            for j in range(2):
                i = tr(PX[:, 128 * j:128 * j + 128], a_ph[:, j, :])
            k = k_phpe[0] = c_pe.up(i)
            wait(act, k, k_pT_free[0])
            spare.free[n] = k_pT[0] = c_act.up(act.copy(a_pT[:, :], PX[:, 0:256]))

        def post_c(b):
            PX, n = spare.take()
            wait(pe, k_pT[0], d_wr)
            for j in range(2):
                i = pe.matmul(PX[:, 8 * j:8 * j + 8], a_pT[:, 128 * j:128 * j + 128], wr[:, :], start=True, stop=True)
            k = k_pT_free[0] = c_pe.up(i)
            wait(dve, k, d_b, k_iota)
            k = spare.free[n] = c_dve.up(dve.tensor_tensor(
                lg[:, 2 * b:2 * b + 2, :], PX[:, 0:16].rearrange("p (t e) -> p t e", t=2),
                brb[:, :].rearrange("p (t e) -> p t e", t=1).broadcast_to((128, 2, NE)), ALU.add))
            if b in ROUTED:
                wait(dve, k)
                k_hot[b] = choose(*ROUTED[b])

        def post_d(b):
            if b not in ROUTED:
                return
            t0, t1 = ROUTED[b]
            n8 = 8 * (t1 - t0)
            PX, n = spare.take()
            wait(pe, k_hot[b], k_tri)
            h = hot[:, 0:t1 - t0, :].rearrange("p t e -> p (t e)")
            pe.matmul(PX[:, 0:n8], tri[:, :], h, start=True, stop=True)
            k = c_pe.up(pe.matmul(PX[:, n8:2 * n8], ones[:, :], h, start=True, stop=True))
            wait(act, k, k_cnt_free[0])
            spare.free[n] = k_cnt[b] = c_act.up(act.copy(cnt[:, 0:2 * n8], PX[:, 0:2 * n8]))

        k_cnt, k_cnt_free = {}, [None]

        def post_e(b):
            if b in ROUTED:
                k_cnt_free[0] = place(*ROUTED[b], k_cnt[b], k_xn[b])
                while to_send and b >= NB - 2:
                    send()

        n_u = 8 * NB
        VALUES = {0: (0, 0), 2: (0, 1)}
        for b in range(NB):
            VALUES |= {8 * b + 1: (b, 2), 8 * b + 3: (b, 3)}
            if b:
                VALUES |= {8 * b - 2: (b, 0), 8 * b - 1: (b, 1)}
        LAST = {n_u + 1: (0, 1, 2, 3), n_u + 2: (4,), n_u + 3: (5,), n_u + 4: (6, 7)}
        POST = ((14, post_a), (15, post_a2), (15, post_b), (16, post_c), (17, post_d), (18, post_e))

        def at(s, lag):
            b, c = divmod(s - lag, 8)
            return b if c == 0 and 0 <= b < NB else None

        pre_a(0)
        first()
        pre_a2(0)
        pre_b(0)
        second()
        if stage_b:
            pre_c(0)
        for s in range(n_u + 12):
            if s > n_u:
                if s < n_u + 3:
                    weigh(s - 3)
                if s < n_u + 2:
                    expo(s - 2)
            if 5 <= s < n_u + 5:
                keep(s - 5)
            if s < n_u:
                T(s)
            if s in VALUES:
                values(*VALUES[s])
            if 4 <= s < n_u + 4:
                TR(s - 4)
            if 3 <= s <= n_u:
                weigh(s - 3)
                send()
            if 2 <= s <= n_u:
                expo(s - 2)
            if 1 <= s <= n_u:
                S(s - 1)
            for lag, what in ((-7, pre_a), (-5, pre_a2), (-4, pre_b), (-3, pre_c if stage_b else None)):
                b = at(s, lag)
                if b and what:
                    what(b)
            if (b := at(s, 12)) is not None:
                if b < NB - 1:
                    out(b)
            if s in LAST:
                out_last(*LAST[s])
            if (b := at(s, 13)) is not None and b < NB - 1:
                out_2(b)
            if 4 <= s < n_u + 4:
                PV(s - 4)
            for lag, what in POST:
                if (b := at(s, lag)) is not None:
                    what(b)
            extra(s, k_mn.get(2 * n_u - 1))

    def V(i):
        k = c_dve.up(i)
        wait(dve, k)
        return k

    def start_rows():
        V(dve.tensor_scalar(run[:, :], iota_s[:, 0:NE], float(REG), None, ALU.mult))

    ROUTED = {1: (0, 4), 3: (4, 8), 5: (8, 12), 6: (12, 14), 7: (14, 16)}

    def by_tile(a, n):
        return a.rearrange("p (t e) -> p t e", e=1).broadcast_to((128, n, NE))

    def by_expert(a, n):
        return a.rearrange("p (t e) -> p t e", t=1).broadcast_to((128, n, NE))

    def choose(t0, t1):
        n = t1 - t0
        l, h, g = lg[:, t0:t1, :], hot[:, 0:n, :], gmx[:, 0:n]
        V(dve.tensor_reduce(g, l, AX, ALU.max))
        V(dve.tensor_tensor(h, l, by_tile(g, n), ALU.is_ge))
        V(dve.tensor_tensor(h, h, by_expert(iota_e[:, :], n), ALU.mult))
        V(dve.tensor_reduce(g, h, AX, ALU.max))
        return V(dve.tensor_tensor(h, h, by_tile(g, n), ALU.is_equal))

    def place(t0, t1, k, k_rows):
        n = t1 - t0
        c = cnt[:, 0:16 * n].rearrange("p (a t e) -> p a t e", a=2, e=NE)
        wait(dve, k)
        V(dve.tensor_copy(bas[:, 0, :], run[:, :]))
        for j in range(1, n + 1):
            V(dve.tensor_tensor(bas[:, j, :] if j < n else run[:, :], c[:, 1, j - 1, :], bas[:, j - 1, :], ALU.add))
        b = bas[:, 0:n, :]
        k0 = V(dve.tensor_tensor(b, c[:, 0, :, :], b, ALU.add))
        V(dve.tensor_tensor(b, b, hot[:, 0:n, :], ALU.mult))
        V(dve.tensor_reduce(posf[:, 0:n], b, AX, ALU.add))
        k1 = V(dve.tensor_copy(posi[:, t0:t1], posf[:, 0:n]))
        to_send.extend((j, k1, k_rows) for j in range(t0, t1))
        return k0

    to_send = []

    def send():
        if to_send:
            j, *marks = to_send.pop(0)
            wait(pool, *marks, k_tok)
            d_row[0] = c_sc.up(pool.indirect_dma_start(
                xs_dram, bass.IndirectOffsetOnAxis(ap=posi[:, j:j + 1].bitcast(U32), axis=0), xn[:, j, :], None))

    def gates():
        E3 = lambda a: by_tile(a, NT)
        V(dve.tensor_reduce(gate[:, :], lg[:, :, :], AX, ALU.max))
        k = V(dve.tensor_tensor(f_sub[:, :, :], lg[:, :, :], E3(gate[:, :]), ALU.subtract))
        wait(act, k)
        k = c_act.up(act.activation(f_sub[:, :, :], f_sub[:, :, :], ACT.Exp))
        wait(dve, k)
        V(dve.tensor_reduce(gate[:, :], f_sub[:, :, :], AX, ALU.add))
        V(dve.reciprocal(gate[:, :], gate[:, :]))

    def experts(fill_pe, fill):
        V(dve.tensor_copy(runi[:, :], run[:, :]))
        k_run = (c_dve, c_dve.n)
        d_pad = [None, None]
        for e in range(NE):
            q = (sp, act, pool)[e % 3]
            wait(q, k_run, k_padt)
            r = q.value_load(runi[0:1, e:e + 1], min_val=0, max_val=NE * REG)
            d_pad[q is pool] = (c_pad2 if q is pool else c_pad).up(q.dma_start(xs_dram[bass.ds(r, 128), :], padt[:, :]))
        tot = f_e[0]
        V(dve.scalar_tensor_tensor(tot[:, :], iota_s[:, 0:NE], -float(REG), run[:, :], ALU.mult, ALU.add))
        V(dve.tensor_tensor(f_k16[:, :, :], tot[:, :].rearrange("p (e k) -> p e k", k=1).broadcast_to((128, NE, 16)),
                            iota_k[:, :].rearrange("p (e k) -> p e k", e=1).broadcast_to((128, NE, 16)), ALU.is_gt))
        V(dve.tensor_reduce(f_e[1][:, :], f_k16[:, :, :], AX, ALU.add))
        a, o = f_e[1], [f_e[2], f_e[3], f_e[4]]
        for n, d in enumerate((1, 2, 4)):
            dve.tensor_copy(o[n][:, 0:d], a[:, 0:d])
            V(dve.tensor_tensor(o[n][:, d:], a[:, d:], a[:, 0:NE - d], ALU.add))
            a = o[n]
        V(dve.tensor_scalar(f_e[5][:, :], f_e[1][:, :], -128.0, float(REG), ALU.mult, ALU.add))
        V(dve.tensor_tensor(f_g[:, :, :], iota_s[:, :].rearrange("p (s e) -> p s e", e=1).broadcast_to((128, NS, NE)),
                            a[:, :].rearrange("p (s e) -> p s e", s=1).broadcast_to((128, NS, NE)), ALU.is_ge))
        V(dve.tensor_tensor(f_g2[:, :, :], f_g[:, :, :],
                            f_e[5][:, :].rearrange("p (s e) -> p s e", s=1).broadcast_to((128, NS, NE)), ALU.mult))
        V(dve.tensor_reduce(f_row[:, :], f_g2[:, :, :], AX, ALU.add))
        V(dve.scalar_tensor_tensor(f_row[:, :], iota_s[:, :], 128.0, f_row[:, :], ALU.mult, ALU.add))
        k_row = V(dve.tensor_copy(f_ri[:, :], f_row[:, :]))
        c_xs = [dma_sem() for _ in range(6)]
        groups = [(4 * g, min(4 * g + 4, NS)) for g in range(6)]
        d_xs = []
        for g, (a0, a1) in enumerate(groups):
            where = []
            for s in range(a0, a1):
                q = act if s < 8 and s % 2 else sp
                wait(q, k_row)
                where.append((s, q, q.value_load(f_ri[0:1, s:s + 1], min_val=0, max_val=XROWS - 128)))
            for s, q, r in where:
                wait(q, d_row[0], *d_pad, d_empty)
                d = c_xs[g].up(q.dma_start(f_xs[:, s, :], xs_dram[bass.ds(r, 128), :]))
            d_xs.append(d)
        V(dve.memset(f_ef[:, NS:NS + 1], 0.0))
        V(dve.tensor_reduce(f_ef[:, 0:NS], f_g[:, :, :], AX, ALU.add))
        V(dve.tensor_scalar(f_ef[:, :], f_ef[:, :], float(NE - 1), None, ALU.min))
        k_ei = V(dve.tensor_copy(f_ei[:, :], f_ef[:, 0:NS]))
        wait(dve, k_pid)
        k_sel = V(dve.tensor_scalar(f_sel[:, :], f_ef[:, :], pid[:, 0:1], None, ALU.is_equal))
        fill_pe()
        k_x, k_h, k_th, k_y = {}, {}, {}, {}
        k_hm, k_sum, k_high, k_ht, k_ym = {}, {}, {}, {}, {}
        wait(pe, k_ei)

        wait(pe, k_sel, k_fb[0])
        for f in range(4):
            i = pe.matmul(ps[7][:, 32 * f:32 * f + NS + 1], b1s[:, 128 * f:128 * f + 128], f_sel[:, :],
                          start=True, stop=True)
        k = c_pe.up(i)
        wait(act, k)
        k_b1 = c_act.up(act.copy(f_b1[:, :, :], ps[7][:, 0:128].rearrange("p (f s) -> p f s", f=4)[:, :, 0:NS]))

        def XT(g):
            a0, a1 = groups[g]
            bank = ps[g % 2]
            wait(pe, d_xs[g], k_x.get(g - 2, (None, k_ei))[1])
            for s in range(a0, a1):
                i = tr(bank[:, 128 * (s - a0):128 * (s - a0) + 128], f_xs[:, s, 0:128])
            k = c_pe.up(i)
            n = 128 * (a1 - a0)
            k_x[g] = split(f_xth[g % 2][:, 0:n], f_xtl[g % 2][:, 0:n], bank[:, 0:n],
                           [k, k_hm.get(4 * (g - 2) + 3)])

        def H(s):
            g, j = divmod(s, 4)
            bank = ps[2 + s % 2]
            r = slice(128 * j, 128 * j + 128)
            e = pe.value_load(f_ei[0:1, s:s + 1], min_val=0, max_val=NE - 1)
            wait(pe, *k_x[g], k_h.get(s - 2), k_ff[0])
            wh, wl = w1h[:, bass.ds(e * 512, 512)], w1l[:, bass.ds(e * 512, 512)]
            i = three(bank[:, :], f_xth[g % 2][:, r], f_xtl[g % 2][:, r], wh, wl)
            k = k_hm[s] = c_pe.up(i)
            wait(act, k, k_th.get(s - 2))
            k_h[s] = c_act.up(act.copy(f_h[s % 2][:, :], bank[:, :]))

        def HT(s):
            bank = ps[4 + s % 2]
            wait(pe, k_h[s], k_sum.get(s - 2))
            for f in range(4):
                i = tr(bank[:, 128 * f:128 * f + 128], f_h[s % 2][:, 128 * f:128 * f + 128])
            k = k_th[s] = c_pe.up(i)
            h2 = f_h2[s % 2]
            wait(dve, k, k_b1, *k_ht.get(s - 2, ()))
            k_sum[s] = c_dve.up(dve.tensor_tensor(
                h2[:, :].rearrange("p (f n) -> p f n", f=4), bank[:, :].rearrange("p (f n) -> p f n", f=4),
                f_b1[:, :, s:s + 1].broadcast_to((128, 4, 128)), ALU.add))

        def relu(s):
            h2, high = f_h2[s % 2], f_hth[s % 3]
            wait(act, k_sum[s], k_ym.get(s - 3))
            k_high[s] = c_act.up(act.activation(high[:, :], h2[:, :], ACT.Relu))

        def relu_low(s):
            h2, high, a = f_h2[s % 2], f_hth[s % 3], k_high[s]
            wait(dve, a, k_ym.get(s - 3))
            k_ht[s] = a, c_dve.up(dve.scalar_tensor_tensor(f_htl[s % 3][:, :], h2[:, :], 0.0, high[:, :].bitcast(F32),
                                                           ALU.max, ALU.subtract))

        def Y(s):
            bank = ps[6 + s % 2]
            e = pe.value_load(f_ei[0:1, s:s + 1], min_val=0, max_val=NE - 1)
            wait(pe, *k_ht[s], k_y.get(s - 2), k_b1)
            o = bank[:, 0:128]
            for f in range(4):
                r = slice(128 * f, 128 * f + 128)
                pe.matmul(bank[:, 0:256], f_hth[s % 3][:, r],
                          w2[:, bass.ds(e * 4 + f, 1), :].rearrange("p a n -> p (a n)"), start=(f == 0), stop=False)
                pe.matmul(o, f_htl[s % 3][:, r],
                          w2[:, bass.ds(e * 4 + f, 1), 0:128].rearrange("p a n -> p (a n)"), start=False, stop=False)
            i = pe.matmul(o, f_sel[:, s:s + 1].broadcast_to((128, 128)), b2s[:, :], start=False, stop=True)
            k = k_ym[s] = c_pe.up(i)
            wait(dve, k)
            k_y[s] = c_dve.up(dve.tensor_reduce(f_ys[:, s, :], bank[:, 0:256].rearrange("p (h d) -> p d h", h=2),
                                                AX, ALU.add))

        def back(s):
            wait(pool, k_y[s])
            return c_ys.up(pool.indirect_dma_start(
                ys_dram, bass.IndirectOffsetOnAxis(ap=f_xs[:, s, 128:129].bitcast(U32), axis=0), f_ys[:, s, :], None,
                bounds_check=NT * 128 - 1, oob_is_err=False))

        XT(0)
        for s in range(NS + 3):
            if 2 <= s < NS + 2:
                relu(s - 2)
            if s < NS:
                H(s)
            if s == 0:
                XT(1)
            if 1 <= s <= NS:
                HT(s - 1)
            if 2 <= s < NS + 2:
                relu_low(s - 2)
            if s == 4:
                fill()
            if s == 8:
                gates()
            if s >= 3:
                Y(s - 3)
                d = back(s - 3)
            if s % 4 == 3 and s // 4 + 2 < 6:
                XT(s // 4 + 2)
        ysv = ys_dram.rearrange("(s p) d -> p s d", p=128)
        d_yt = [load(xn[:, 4 * g:4 * g + 4, 0:128], ysv[:, 4 * g:4 * g + 4, :], eng=(sp, act)[g % 2], after=[d])
                for g in range(4)]
        for eng in (pe, dve, act, pool, sp):
            wait(eng, d)
        barrier()

        def add(j):
            wait(dve, d_yt[j // 4])
            return c_dve.up(dve.scalar_tensor_tensor(x[:, j, :], xn[:, j, 0:128], gate[:, j:j + 1], x[:, j, :],
                                                     ALU.mult, ALU.add))

        return add

    def all_done():
        return [(c, c.n) for c in (c_pe, c_dve, c_act, c_pool) if c.n]

    def barrier():
        m = all_done()
        for eng in (pe, dve, act, pool, sp):
            wait(eng, *m)

    wait(dve, k_iota)
    start_rows()

    d_b_w, k_bT, k_wb = [], [None], []

    def extra_a(s, table_free):
        if s % 3 == 0 and s // 3 < 16:
            stage_load(s // 3)
        if s % 3 == 1 and s // 3 < 16:
            stage_split(s // 3)
        if s % 3 == 2 and s // 3 < 16:
            stage_low(s // 3)
        if s == 50:
            stage_bias(t["b1"], b1s, 512)
        if s == 56:
            stage_bias(t["b2"], b2s, 128)
        if s == 64:
            d_b_w.append(load(bq[:, :], t["w_q"], after=[table_free]))
            d_b_w.append(load(bu[:, :], t["w_kv_up"]))
            d_b_w.append(load(bkd[:, :], t["w_kv_down"]))
            d_b_w.append(load(bo[:, :, :], t["w_out_b"].rearrange("(c p) n -> p c n", p=128)))
        if s in (3, 4):
            weights_a3(s - 3)
        if s in (66, 67):
            src, dst, d = ((bq, bqT, d_b_w[0]) if s == 66 else (bu, bkT, d_b_w[1]))
            for g in range(2):
                bank, n = spare.take()
                wait(pe, d)
                for j in range(4):
                    i = tr(bank[:, 128 * j:128 * j + 128], src[:, 512 * g + 128 * j:512 * g + 128 * j + 128])
                k = c_pe.up(i)
                wait(act, k)
                k = spare.free[n] = k_bT[0] = c_act.up(
                    act.copy(dst[:, 4 * g:4 * g + 4, :], bank[:, :].rearrange("p (a b) -> p a b", a=4)))

    TA = a_TA

    def table_a(h, it):
        if it == 1:
            return TA[:, 256 * h:256 * h + 256]
        o = TA[:, 256 * h + 128:256 * h + 256]
        return bass.AP(o.tensor, o.offset, [list(o.ap[0]), [4096 - 256 * h - 128, 2], [1, 128]])

    attention(False, lambda b: d_x if b else d_x0, lambda n: k_ma[n], k_va, k_oa, table_a, bias_ready, extra_a,
              weights_a1, weights_a2)
    barrier()

    def products_b():
        wait(pe, k_bT[0])
        for p in range(4):
            k_wb.extend(product(bqT, bkT, p, ps[2 + p]))

    def weights_b():
        k_wb.extend(split(wvh[:, :], wvl[:, :], bu[:, 1024:2048], [d_b_w[1]]))
        k_wb.extend(split(wo[:, :, 0:128], wo[:, :, 128:256], bo[:, :, :], [d_b_w[3]]))
        k_wb.extend(split(kdh[:, :], kdl[:, :], bkd[:, :], [d_b_w[2]]))

    add = experts(products_b, weights_b)

    def ready_b(b):
        add(2 * b)
        return add(2 * b + 1)

    start_rows()

    CM = b_cm[:, :]
    k = c_pool.up(pool.memset(CM, 0.0))
    wait(pool, k)
    k_cm = c_pool.up(pool.affine_select(out=CM, in_=CM, compare_op=ALU.is_ge, fill=MASKED, base=128,
                                        pattern=[[-1, 256]], channel_multiplier=1))
    attention(True, ready_b, lambda n: (), k_wb, (), lambda h, it: CM if it == 1 else CM[:, 128:256],
              lambda u: k_cm, lambda s, k: None, lambda: None, lambda: None)
    barrier()
    c_o = dma_sem()
    last = []

    add = experts(lambda: None, lambda: None)
    for j in range(NT):
        k = add(j)
        if j % 4 == 3:
            last.append(load(ov[:, j - 3:j + 1, :], x[:, j - 3:j + 1, :], after=[k], c=c_o))
    wait(sp, last[-1])
    ctx.close()


_INS = ["L0_attn_a_x", "L0_attn_a_w_qkv", "L0_attn_a_w_out", "L0_attn_b_w_kv_down", "L0_attn_b_w_kv_up",
        "L0_attn_b_w_q", "L0_attn_b_w_out", "L0_ffn_Wr", "L0_ffn_br", "L0_ffn_ln_g", "L0_ffn_ln_b",
        "L0_ffn_W1", "L0_ffn_b1", "L0_ffn_W2", "L0_ffn_b2"]
_SHORT = {"L0_attn_a_x": "x", "L0_attn_a_w_qkv": "w_qkv", "L0_attn_a_w_out": "w_out_a",
          "L0_attn_b_w_kv_down": "w_kv_down", "L0_attn_b_w_kv_up": "w_kv_up", "L0_attn_b_w_q": "w_q",
          "L0_attn_b_w_out": "w_out_b", "L0_ffn_Wr": "Wr", "L0_ffn_br": "br", "L0_ffn_ln_g": "ln_g",
          "L0_ffn_ln_b": "ln_b", "L0_ffn_W1": "W1", "L0_ffn_b1": "b1", "L0_ffn_W2": "W2", "L0_ffn_b2": "b2"}


def kernel(**inputs):
    import concourse.bacc as bacc
    from concourse.bass_utils import run_bass_kernel_spmd

    nc = bacc.Bacc("TRN2", target_bir_lowering=False, num_devices=1)
    arrays, t = {}, {}

    def give(name, a):
        arrays[f"in_{name}"] = a
        t[name] = nc.dram_tensor(f"in_{name}", a.shape, mybir.dt.from_np(a.dtype), kind="ExternalInput").ap()

    for name in _INS:
        a = np.ascontiguousarray(inputs[name])
        give(_SHORT[name], a)
    rel = np.ascontiguousarray(inputs["L0_attn_a_rel_bias"])
    index = np.minimum(127 + np.arange(256)[None, :] - np.arange(128)[:, None], 254)
    give("bias", np.ascontiguousarray(rel[index].transpose(0, 2, 1)))
    t["out"] = nc.dram_tensor("out_0", (8, 256, 128), F32, kind="ExternalOutput").ap()
    build(nc, t)
    r = run_bass_kernel_spmd(nc, [arrays], core_ids=[0])
    return r.results[0]["out_0"]
```
